# Optimizing a Trainium2 kernel written in Bass

```python
import numpy as np
import jax
import jax.numpy as jnp

def _softmax(x, axis=-1):
    return jax.nn.softmax(x, axis=axis)

def _gelu(x):
    return jax.nn.gelu(x, approximate=True)

def _silu(x):
    return jax.nn.silu(x)

def _sigmoid(x):
    return jax.nn.sigmoid(x)

def _layernorm(x, axis=-1, eps=1e-05):
    m = jnp.mean(x, axis=axis, keepdims=True)
    v = jnp.var(x, axis=axis, keepdims=True)
    return (x - m) / jnp.sqrt(v + eps)

def _scatter_add(tgt, idx, src, axis=0):
    return tgt.at[idx].add(src)

def _segment_sum(src, seg, n):
    return jax.ops.segment_sum(src, seg, n)
kernel_name = 'mk_decoder_postln_d1_seqx_r4_bb5627'

def setup_inputs(seed: int=0):
    np.random.seed(seed)
    _w = jnp.asarray

    def _rec_inputs():
        import jax
        import jax.numpy as jnp
        _rk = jax.random.key(seed)
        x = 7.22e-05 + 1 * jax.random.normal(jax.random.fold_in(_rk, 1), (32, 256, 256), jnp.float32)
        _lenS = 256 - jax.random.randint(jax.random.fold_in(_rk, 7), (32,), 0, max(1, 256 // 4) + 1, jnp.int32)
        _lenS2 = 77 - jax.random.randint(jax.random.fold_in(_rk, 8), (32,), 0, max(1, 77 // 4) + 1, jnp.int32)
        _ctx_1024P = jax.random.normal(jax.random.fold_in(_rk, 11), (32, 16, 256), jnp.float32)
        _ctx_1024c = jax.random.dirichlet(jax.random.fold_in(_rk, 511), 0.3 * jnp.ones((16,), jnp.float32), (32, 77))
        _ctx_1024t = jnp.einsum('bsk,bkd->bsd', _ctx_1024c, _ctx_1024P)
        _ctx_1024t = _ctx_1024t * jax.lax.rsqrt(jnp.mean(jnp.square(_ctx_1024t)) + 1e-12) * 0.953939
        ctx_1024 = 4.13588e-05 + 0.999923 * (_ctx_1024t + 0.3 * jax.random.normal(jax.random.fold_in(_rk, 611), (32, 77, 256), jnp.float32))
        return (x, ctx_1024)
    x, ctx_1024 = _rec_inputs()

    def _L0_attn_setup():
        import jax, jax.numpy as jnp
        import numpy as np
        DIM = 256
        D_STATE = 64
        D_CONV = 4
        EXPAND = 2
        N_HEADS = 8
        D_INNER = DIM * EXPAND
        HEAD_DIM = D_INNER // N_HEADS
        D_IN_PROJ = D_INNER + D_INNER + N_HEADS + D_STATE + D_STATE
        BATCH, SEQ = (2, 256)
        EPS = 1e-06

        def _rms_norm(y, w):
            rms = jnp.sqrt(jnp.mean(y * y, axis=-1, keepdims=True) + EPS)
            return y / rms * w

        def _depthwise_causal_conv(u, w, b):
            L = u.shape[1]
            up = jnp.pad(u, ((0, 0), (D_CONV - 1, 0), (0, 0)))
            out = b[None, None, :]
            for k in range(D_CONV):
                out = out + up[:, k:k + L, :] * w[None, None, :, k]
            return out

        def _mamba2_forward(x, in_proj_w, conv_w, conv_b, A_log, D_param, dt_bias, norm_w, out_proj_w):
            B_sz, L, _ = x.shape
            zxBCdt = x @ in_proj_w.T
            z, xc, Bm, Cm, dt = jnp.split(zxBCdt, [D_INNER, 2 * D_INNER, 2 * D_INNER + N_HEADS, 2 * D_INNER + N_HEADS + D_STATE], axis=-1)
            xc = _depthwise_causal_conv(xc, conv_w, conv_b)
            xc = jax.nn.silu(xc)
            xh = xc.reshape(B_sz, L, N_HEADS, HEAD_DIM)
            A = -jnp.exp(A_log)
            dt = jax.nn.softplus(Bm + dt_bias)
            a_bar = jnp.exp(dt * A[None, None, :])

            def step(h, t):
                a_t, b_t, c_t, x_t = t
                h = a_t[:, :, None, None] * h + b_t[:, None, None, :] * x_t[..., None]
                y_t = jnp.einsum('bhdn,bn->bhd', h, c_t)
                return (h, y_t)
            h0 = jnp.zeros((B_sz, N_HEADS, HEAD_DIM, D_STATE), dtype=x.dtype)
            xs = (jnp.moveaxis(a_bar, 1, 0), jnp.moveaxis(Cm, 1, 0) * 0 + jnp.moveaxis(Cm, 1, 0), jnp.moveaxis(dt, 1, 0) * 0, jnp.moveaxis(xh, 1, 0))
            B_proj, C_proj = (Cm, dt if False else (Cm, None))
            raise NotImplementedError
        key = jax.random.key(seed)
        ks = jax.random.split(key, 9)
        x = jax.random.normal(ks[0], (BATCH, SEQ, DIM), dtype=jnp.float32)
        in_proj_w = jax.random.normal(ks[1], (D_IN_PROJ, DIM), dtype=jnp.float32) * 0.02
        conv_w = jax.random.normal(ks[2], (D_INNER, D_CONV), dtype=jnp.float32) * 0.2
        conv_b = jax.random.normal(ks[3], (D_INNER,), dtype=jnp.float32) * 0.02
        A_log = jax.random.normal(ks[4], (N_HEADS,), dtype=jnp.float32) * 0.5
        D_param = jnp.ones((N_HEADS,), dtype=jnp.float32) + 0.1 * jax.random.normal(ks[5], (N_HEADS,), dtype=jnp.float32)
        dt_bias = jax.random.normal(ks[6], (N_HEADS,), dtype=jnp.float32) * 0.5
        norm_w = jnp.ones((D_INNER,), dtype=jnp.float32)
        out_proj_w = jax.random.normal(ks[7], (DIM, D_INNER), dtype=jnp.float32) * 0.02
        return {'x': x, 'in_proj_w': in_proj_w, 'conv_w': conv_w, 'conv_b': conv_b, 'A_log': A_log, 'D_param': D_param, 'dt_bias': dt_bias, 'norm_w': norm_w, 'out_proj_w': out_proj_w}
    _L0_attn_all = _L0_attn_setup()
    _L0_attn_in = {k: v for k, v in _L0_attn_all.items() if k in ('in_proj_w', 'conv_w', 'conv_b', 'A_log', 'D_param', 'dt_bias', 'norm_w', 'out_proj_w')}
    del _L0_attn_all

    def _L0_xattn_setup():
        import jax, jax.numpy as jnp
        import numpy as np
        N, L, E, H, D = (4, 512, 256, 16, 64)
        key = jax.random.key(seed)
        ks = jax.random.split(key, 8)
        s = 1.0 / np.sqrt(E)
        return {'Q': jax.random.normal(ks[0], (N, L, E), jnp.float32), 'K': jax.random.normal(ks[1], (N, L, E), jnp.float32), 'V': jax.random.normal(ks[2], (N, L, E), jnp.float32), 'Wq': jax.random.normal(ks[3], (H * D, E), jnp.float32) * s, 'bq': jnp.zeros((H * D,), jnp.float32), 'Wk': jax.random.normal(ks[4], (H * D, E), jnp.float32) * s, 'bk': jnp.zeros((H * D,), jnp.float32), 'Wv': jax.random.normal(ks[5], (H * D, E), jnp.float32) * s, 'bv': jnp.zeros((H * D,), jnp.float32), 'Wo': jax.random.normal(ks[6], (E, H * D), jnp.float32) * s, 'bo': jnp.zeros((E,), jnp.float32)}
    _L0_xattn_all = _L0_xattn_setup()
    _L0_xattn_in = {k: v for k, v in _L0_xattn_all.items() if k in ('Wq', 'bq', 'Wk', 'bk', 'Wv', 'bv', 'Wo', 'bo')}
    del _L0_xattn_all

    def _L0_ffn_setup():
        import jax, jax.numpy as jnp
        import numpy as np
        E, K, D = (8, 2, 256)
        B, S = (2, 1024)

        def _layernorm(x, g, b, eps=1e-06):
            m = jnp.mean(x, axis=-1, keepdims=True)
            v = jnp.var(x, axis=-1, keepdims=True)
            return (x - m) * jax.lax.rsqrt(v + eps) * g + b
        key = jax.random.key(seed)
        ks = jax.random.split(key, 6)
        n = lambda k, shape, scale: jax.random.normal(k, shape, jnp.float32) * scale
        return {'x': n(ks[0], (B, S, D), 1.0), 'gate_w': n(ks[1], (D, E), 0.02), 'w1': n(ks[2], (E, D, 2 * D), 0.02), 'b1': jnp.zeros((E, 2 * D), jnp.float32), 'w2': n(ks[3], (E, 2 * D, D), 0.02), 'b2': jnp.zeros((E, D), jnp.float32), 'ln_g': jnp.ones((E, D), jnp.float32), 'ln_b': jnp.zeros((E, D), jnp.float32)}
    _L0_ffn_all = _L0_ffn_setup()
    _L0_ffn_in = {k: v for k, v in _L0_ffn_all.items() if k in ('gate_w', 'w1', 'b1', 'w2', 'b2', 'ln_g', 'ln_b')}
    del _L0_ffn_all
    return {'x': x, 'ctx_1024': ctx_1024, 'L0_attn_in_proj_w': _L0_attn_in['in_proj_w'], 'L0_attn_conv_w': _L0_attn_in['conv_w'], 'L0_attn_conv_b': _L0_attn_in['conv_b'], 'L0_attn_A_log': _L0_attn_in['A_log'], 'L0_attn_D_param': _L0_attn_in['D_param'], 'L0_attn_dt_bias': _L0_attn_in['dt_bias'], 'L0_attn_norm_w': _L0_attn_in['norm_w'], 'L0_attn_out_proj_w': _L0_attn_in['out_proj_w'], 'L0_xattn_Wq': _L0_xattn_in['Wq'], 'L0_xattn_bq': _L0_xattn_in['bq'], 'L0_xattn_Wk': _L0_xattn_in['Wk'], 'L0_xattn_bk': _L0_xattn_in['bk'], 'L0_xattn_Wv': _L0_xattn_in['Wv'], 'L0_xattn_bv': _L0_xattn_in['bv'], 'L0_xattn_Wo': _L0_xattn_in['Wo'], 'L0_xattn_bo': _L0_xattn_in['bo'], 'L0_ffn_gate_w': _L0_ffn_in['gate_w'], 'L0_ffn_w1': _L0_ffn_in['w1'], 'L0_ffn_b1': _L0_ffn_in['b1'], 'L0_ffn_w2': _L0_ffn_in['w2'], 'L0_ffn_b2': _L0_ffn_in['b2'], 'L0_ffn_ln_g': _L0_ffn_in['ln_g'], 'L0_ffn_ln_b': _L0_ffn_in['ln_b']}

def reference(x, ctx_1024, L0_attn_in_proj_w, L0_attn_conv_w, L0_attn_conv_b, L0_attn_A_log, L0_attn_D_param, L0_attn_dt_bias, L0_attn_norm_w, L0_attn_out_proj_w, L0_xattn_Wq, L0_xattn_bq, L0_xattn_Wk, L0_xattn_bk, L0_xattn_Wv, L0_xattn_bv, L0_xattn_Wo, L0_xattn_bo, L0_ffn_gate_w, L0_ffn_w1, L0_ffn_b1, L0_ffn_w2, L0_ffn_b2, L0_ffn_ln_g, L0_ffn_ln_b):
    import jax
    import jax.numpy as jnp

    def _L0_attn_ref(x, in_proj_w, conv_w, conv_b, A_log, D_param, dt_bias, norm_w, out_proj_w):
        import jax, jax.numpy as jnp
        import numpy as np
        DIM = 256
        D_STATE = 64
        D_CONV = 4
        EXPAND = 2
        N_HEADS = 8
        D_INNER = DIM * EXPAND
        HEAD_DIM = D_INNER // N_HEADS
        D_IN_PROJ = D_INNER + D_INNER + N_HEADS + D_STATE + D_STATE
        BATCH, SEQ = (2, 256)
        EPS = 1e-06

        def _rms_norm(y, w):
            rms = jnp.sqrt(jnp.mean(y * y, axis=-1, keepdims=True) + EPS)
            return y / rms * w

        def _depthwise_causal_conv(u, w, b):
            L = u.shape[1]
            up = jnp.pad(u, ((0, 0), (D_CONV - 1, 0), (0, 0)))
            out = b[None, None, :]
            for k in range(D_CONV):
                out = out + up[:, k:k + L, :] * w[None, None, :, k]
            return out

        def _mamba2_forward(x, in_proj_w, conv_w, conv_b, A_log, D_param, dt_bias, norm_w, out_proj_w):
            B_sz, L, _ = x.shape
            zxBCdt = x @ in_proj_w.T
            z, xc, Bm, Cm, dt = jnp.split(zxBCdt, [D_INNER, 2 * D_INNER, 2 * D_INNER + N_HEADS, 2 * D_INNER + N_HEADS + D_STATE], axis=-1)
            xc = _depthwise_causal_conv(xc, conv_w, conv_b)
            xc = jax.nn.silu(xc)
            xh = xc.reshape(B_sz, L, N_HEADS, HEAD_DIM)
            A = -jnp.exp(A_log)
            dt = jax.nn.softplus(Bm + dt_bias)
            a_bar = jnp.exp(dt * A[None, None, :])

            def step(h, t):
                a_t, b_t, c_t, x_t = t
                h = a_t[:, :, None, None] * h + b_t[:, None, None, :] * x_t[..., None]
                y_t = jnp.einsum('bhdn,bn->bhd', h, c_t)
                return (h, y_t)
            h0 = jnp.zeros((B_sz, N_HEADS, HEAD_DIM, D_STATE), dtype=x.dtype)
            xs = (jnp.moveaxis(a_bar, 1, 0), jnp.moveaxis(Cm, 1, 0) * 0 + jnp.moveaxis(Cm, 1, 0), jnp.moveaxis(dt, 1, 0) * 0, jnp.moveaxis(xh, 1, 0))
            B_proj, C_proj = (Cm, dt if False else (Cm, None))
            raise NotImplementedError
        B_sz, L, _ = x.shape
        zxBCdt = x @ in_proj_w.T
        z = zxBCdt[..., :D_INNER]
        xc = zxBCdt[..., D_INNER:2 * D_INNER]
        Bp = zxBCdt[..., 2 * D_INNER:2 * D_INNER + N_HEADS]
        Bm = zxBCdt[..., 2 * D_INNER:2 * D_INNER + N_HEADS]
        Cm = zxBCdt[..., 2 * D_INNER + N_HEADS:2 * D_INNER + N_HEADS + D_STATE]
        dtm = zxBCdt[..., 2 * D_INNER + N_HEADS + D_STATE:]
        dt = jax.nn.softplus(Bm + dt_bias)
        B_proj, C_proj = (Cm, dtm)
        xc = _depthwise_causal_conv(xc, conv_w, conv_b)
        xc = jax.nn.silu(xc)
        xh = xc.reshape(B_sz, L, N_HEADS, HEAD_DIM)
        A = -jnp.exp(A_log)
        a_bar = jnp.exp(dt * A[None, None, :])

        def step(h, t):
            a_t, b_t, c_t, x_t = t
            h = a_t[:, :, None, None] * h + b_t[:, None, None, :] * x_t[..., None]
            y_t = jnp.einsum('bhdn,bn->bhd', h, c_t)
            return (h, y_t)
        h0 = jnp.zeros((B_sz, N_HEADS, HEAD_DIM, D_STATE), dtype=x.dtype)
        ts = (jnp.moveaxis(a_bar, 1, 0), jnp.moveaxis(B_proj, 1, 0), jnp.moveaxis(C_proj, 1, 0), jnp.moveaxis(xh, 1, 0))
        _, ys = jax.lax.scan(step, h0, ts)
        y = jnp.moveaxis(ys, 0, 1)
        y = y + xh * D_param[None, None, :, None]
        y = y.reshape(B_sz, L, D_INNER)
        y = y * jax.nn.silu(z)
        y = _rms_norm(y, norm_w)
        return y @ out_proj_w.T

    def _L0_xattn_ref(Q, K, V, Wq, bq, Wk, bk, Wv, bv, Wo, bo):
        import jax, jax.numpy as jnp
        import numpy as np
        N, L, E, H, D = (4, 512, 256, 16, 64)
        n, lq, e = Q.shape
        lk = K.shape[1]
        q = (Q @ Wq.T + bq).reshape(n, lq, H, D)
        k = (K @ Wk.T + bk).reshape(n, lk, H, D)
        v = (V @ Wv.T + bv).reshape(n, lk, H, D)
        scores = jnp.einsum('nqhd,nkhd->nqkh', q, k) / jnp.sqrt(jnp.float32(D))
        attn = jax.nn.softmax(scores, axis=2)
        out = jnp.einsum('nqkh,nkhd->nqhd', attn, v)
        out = out.reshape(n, lq, H * D)
        return (out @ Wo.T + bo).reshape(n, lq, E)

    def _L0_ffn_ref(x, gate_w, w1, b1, w2, b2, ln_g, ln_b):
        import jax, jax.numpy as jnp
        import numpy as np
        E, K, D = (8, 2, 256)
        B, S = (2, 1024)

        def _layernorm(x, g, b, eps=1e-06):
            m = jnp.mean(x, axis=-1, keepdims=True)
            v = jnp.var(x, axis=-1, keepdims=True)
            return (x - m) * jax.lax.rsqrt(v + eps) * g + b
        orig_shape = x.shape
        xt = x.reshape(-1, orig_shape[-1])
        scores = xt @ gate_w
        ew, ei = jax.lax.top_k(scores, K)
        ew = jax.nn.softmax(ew, axis=-1)
        mask = ei[None, :, :] == jnp.arange(E)[:, None, None]
        wE = jnp.sum(ew[None, :, :] * mask, axis=-1)
        h = jax.nn.gelu(jnp.einsum('td,edf->etf', xt, w1) + b1[:, None, :], approximate=False)
        o = jnp.einsum('etf,efd->etd', h, w2) + b2[:, None, :]
        y = _layernorm(xt[None, :, :] + o, ln_g[:, None, :], ln_b[:, None, :])
        out = jnp.einsum('et,etd->td', wE, y)
        return out.reshape(orig_shape)
    x = _layernorm(x + _L0_attn_ref(x, L0_attn_in_proj_w, L0_attn_conv_w, L0_attn_conv_b, L0_attn_A_log, L0_attn_D_param, L0_attn_dt_bias, L0_attn_norm_w, L0_attn_out_proj_w), axis=-1)
    x = _layernorm(x + _L0_xattn_ref(x, ctx_1024, ctx_1024, L0_xattn_Wq, L0_xattn_bq, L0_xattn_Wk, L0_xattn_bk, L0_xattn_Wv, L0_xattn_bv, L0_xattn_Wo, L0_xattn_bo), axis=-1)
    x = _layernorm(x + _L0_ffn_ref(x, L0_ffn_gate_w, L0_ffn_w1, L0_ffn_b1, L0_ffn_w2, L0_ffn_b2, L0_ffn_ln_g, L0_ffn_ln_b), axis=-1)
    return x

_drawn_inputs = setup_inputs


def setup_inputs(seed=0):
    import zlib

    import numpy as np

    out = dict(_drawn_inputs(seed))
    spreads = {'L0_attn_norm_w': (1.0, 0.2),
     'L0_xattn_bq': (0.0, 0.1),
     'L0_xattn_bk': (0.0, 0.8),
     'L0_xattn_bv': (0.0, 0.1),
     'L0_xattn_bo': (0.0, 0.1),
     'L0_ffn_b1': (0.0, 0.8),
     'L0_ffn_b2': (0.0, 0.1),
     'L0_ffn_ln_g': (1.0, 0.2),
     'L0_ffn_ln_b': (0.0, 0.1)}
    factors = {}
    for name, (base, spread) in spreads.items():
        noise = np.random.default_rng([zlib.crc32(name.encode()), seed]).standard_normal(out[name].shape)
        drawn = base * np.exp(spread * noise) if base else spread * noise
        out[name] = jnp.asarray(drawn.astype(out[name].dtype))
    for name, factor in factors.items():
        out[name] = (out[name] * factor).astype(out[name].dtype)
    return out
```

```python
from contextlib import ExitStack

import numpy as np

import concourse.bass as bass
from concourse import mybir

ALU = mybir.AluOpType
ACT = mybir.ActivationFunctionType
AX = mybir.AxisListType
F32 = mybir.dt.float32
F32R = mybir.dt.float32r
U32 = mybir.dt.uint32

P = 128
D = 256
L = 256
KD = D // P
NT = L // P
PEEL = 4


class Item:

    def __init__(self, half, par):
        self.half, self.par = half, par

    def ago(self, n):
        return Item(self.half + (self.par - n) // 2, (self.par - n) % 2)

    def known(self):
        return isinstance(self.half, int)

    def value(self):
        return 2 * self.half + self.par

    def before(self, n):
        return self.known() and self.value() < n

    def count(self, per, done):
        return self.half * (2 * per) + (self.par * per + done)


def run_steps(eng, n, stages, spare=0):
    last = max(lag for _, lag in stages)

    def peeled(s):
        for stage, lag in stages:
            if 0 <= s - lag < n:
                stage(Item(*divmod(s - lag, 2)))

    for s in range(PEEL):
        peeled(s)
    with eng.Fori(PEEL // 2, (n - spare) // 2) as pair:
        for par in (0, 1):
            for stage, lag in stages:
                stage(Item(pair, par).ago(lag))
    for s in range(n - spare, n + last):
        peeled(s)


def wait_apart(dve, spare, *waits):
    for semaphore, value in waits:
        dve.wait_ge(semaphore, value)
    dve.memset(spare, 0.0)


def split3(eng, out, lhs, rhs, start, stop):
    (lh, ll), (rh, rl) = lhs, rhs
    eng.matmul(out, lh, rh, start=start, stop=False)
    eng.matmul(out, lh, rl, start=False, stop=False)
    return eng.matmul(out, ll, rh, start=False, stop=stop)


def mixer_phase(nc, n_seq, xT, x, x1, w_in, w_out, norm_w, conv_w, conv_b, A_log, D_param, dt_bias, masks):
    H, N_STATE, D_CONV, DI = 8, 64, 4, 512
    HD = DI // H
    MI = DI // P
    C_Z, C_X, C_BC, C_DT = 0, DI, 2 * DI, 2 * DI + 4 * N_STATE
    W_IN = C_DT + H
    RMS_EPS, LN_EPS = 1e-6, 1e-5

    with ExitStack() as ctx:
        def sb(name, shape, dt=F32):
            return ctx.enter_context(nc.sbuf_tensor("a_" + name, shape, dt))

        def sem(name):
            return ctx.enter_context(nc.semaphore("a_" + name))

        w_stage = sb("w_stage", [P, KD, W_IN])
        w_hi = sb("w_hi", [P, KD, C_DT], F32R)
        w_lo = sb("w_lo", [P, KD, C_DT], F32R)
        wo_stage = sb("wo_stage", [P, MI, D])
        wo_hi = sb("wo_hi", [P, MI, D], F32R)
        wo_lo = sb("wo_lo", [P, MI, D], F32R)
        nw = sb("nw", [P, MI])
        cw = sb("cw", [P, MI, D_CONV])
        cb = sb("cb", [P, MI])
        a_neg = sb("a_neg", [P, H])
        d_b = sb("d_b", [P, H])
        dtb = sb("dtb", [P, H])
        mk = sb("mk", [P, 3, P])
        upto, after, ident = mk[:, 0, :], mk[:, 1, :], mk[:, 2, :]
        spare = sb("spare", [P, 1])
        pow_half = sb("pow_half", [P, NT])
        rms_eps = sb("rms_eps", [P, NT])
        ln_eps = sb("ln_eps", [P, NT])

        xT_f = sb("xT_f", [P, 2, KD, L])
        xT_hi = sb("xT_hi", [P, 2, KD, L], F32R)
        xT_lo = sb("xT_lo", [P, 2, KD, L], F32R)
        x_f = sb("x_f", [P, 2, NT, D])
        xc_pad = sb("xc_pad", [P, MI, L + D_CONV - 1])
        conv = sb("conv", [P, MI, L])
        conv_t = sb("conv_t", [P, MI, L])
        sx = sb("sx", [P, 2, MI, L])
        z_t = sb("z_t", [P, NT, DI])
        zs = sb("zs", [P, 2, NT, DI])
        bc = sb("bc", [N_STATE, 2, 2, L])
        v_dt = sb("v_dt", [P, NT * H])
        v_na = sb("v_na", [P, NT * H])
        v_ex = sb("v_ex", [P, NT * H])
        v_ln = sb("v_ln", [P, NT * H])
        v_sp = sb("v_sp", [P, NT * H])
        l_dt = sb("l_dt", [P, 2, NT * H])
        lm = sb("lm", [P, NT, H, P])
        g_m = sb("g_m", [P, 3, P])
        e_x = sb("e_x", [P, NT, H, P])
        mt = sb("mt", [P, NT, H, P])
        x_t = sb("x_t", [P, NT, DI])
        xd = sb("xd", [P, NT, DI])
        cx = sb("cx", [P, DI])
        rc = sb("rc", [P, 2 * H])
        t1 = sb("t1", [P, NT, DI])
        off_r = sb("off_r", [P, DI])
        t2 = sb("t2", [P, DI])
        y = sb("y", [P, 2, NT, DI])
        sq = sb("sq", [P, DI])
        ss = sb("ss", [P, 2, NT])
        ms = sb("ms", [P, NT])
        rinv = sb("rinv", [P, 2, NT])
        yT_hi = sb("yT_hi", [P, MI, L], F32R)
        yT_lo = sb("yT_lo", [P, MI, L], F32R)
        res = sb("res", [P, NT, D])
        st = sb("st", [P, NT, 6])
        mv = sb("mv", [P, NT, 2])
        ve = sb("ve", [P, NT])
        rstd = sb("rstd", [P, NT])
        x1_t = sb("x1_t", [P, 2, NT, D])

        p01 = ctx.enter_context(nc.psum_tensor("a_p01", [P, 2, 512], F32))
        p23 = ctx.enter_context(nc.psum_tensor("a_p23", [P, 2, 512], F32))
        p45 = ctx.enter_context(nc.psum_tensor("a_p45", [P, 2, 512], F32))
        p6 = ctx.enter_context(nc.psum_tensor("a_p6", [P, 512], F32))
        p7 = ctx.enter_context(nc.psum_tensor("a_p7", [P, 512], F32))
        ps_xc = p01[:, :, :].rearrange("p b (m t) -> p (b m) t", m=2)
        ps_yT = p23[:, :, :].rearrange("p b (m t) -> p (b m) t", m=2)
        ps_bc = p6[:, :].rearrange("p (w t) -> p w t", w=2)
        ps_out = p6[:, :].rearrange("p (c d) -> p c d", c=NT)
        ps_g = p7[:, 0:3 * P].rearrange("p (g t) -> p g t", g=3)
        ps_dt = p7[:, 3 * P:3 * P + NT * H]
        ps_rc = p7[:, 3 * P + NT * H:3 * P + NT * H + 2 * H]

        s_load = sem("load")
        s_wprep = sem("wprep")
        s_wout = sem("wout")
        s_aexp = sem("aexp")
        s_pow = sem("pow")
        s_xT_in = [sem("xT_in0"), sem("xT_in1")]
        s_x_in = [sem("x_in0"), sem("x_in1")]
        s_x1_out = [sem("x1_out0"), sem("x1_out1")]
        s_xc, s_z, s_yT, s_bc, s_small, s_g, s_E, s_T, s_out, s_Y, s_off = (
            sem(n) for n in ("xc", "z", "yT", "bc", "small", "g", "E", "T", "out", "Y", "off"))
        s_pad, s_tap, s_sq, s_yhi, s_zt, s_bcc, s_rc, s_exp, s_xt, s_ct, s_dex, s_dln = (
            sem(n) for n in ("pad", "tap", "sq", "yhi", "zt", "bcc", "rc", "exp", "xt", "ct", "dex", "dln"))
        s_xhi, s_conv, s_ylo, s_zs, s_v, s_na, s_gm, s_mt, s_sx, s_sp, s_l, s_res, s_st, s_mv, s_x1, s_t1, s_or = (
            sem(n) for n in ("xhi", "conv", "ylo", "zs", "v", "na", "gm", "mt", "sx", "sp", "l", "res", "st",
                             "mv", "x1", "t1", "or"))
        s_xlo, s_cx, s_xd, s_lm, s_t2, s_y, s_ms, s_ri, s_ve, s_rs = (
            sem(n) for n in ("xlo", "cx", "xd", "lm", "t2", "y", "ms", "ri", "ve", "rs"))

        N_LOADS = 9

        block = ctx.enter_context(nc.Block())

        @block.sync
        def _(sp):
            sp.dma_start(w_stage[:, :, :], w_in.rearrange("(k p) n -> p k n", p=P)).then_inc(s_load, 16)
            sp.dma_start(wo_stage[:, :, :], w_out.rearrange("(k p) n -> p k n", p=P)).then_inc(s_load, 16)
            sp.dma_start(nw[:, :], norm_w).then_inc(s_load, 16)
            sp.dma_start(cw[:, :, :], conv_w).then_inc(s_load, 16)
            sp.dma_start(cb[:, :], conv_b).then_inc(s_load, 16)
            sp.dma_start(a_neg[:, :], A_log.partition_broadcast(P)).then_inc(s_load, 16)
            sp.dma_start(d_b[:, :], D_param.partition_broadcast(P)).then_inc(s_load, 16)
            sp.dma_start(dtb[:, :], dt_bias.partition_broadcast(P)).then_inc(s_load, 16)
            sp.dma_start(mk[:, :, :], masks).then_inc(s_load, 16)

            def load_xT(b):
                if not b.before(2):
                    sp.wait_ge(s_xhi, b.ago(2).count(1, 1))
                    sp.wait_ge(s_xlo, b.ago(2).count(1, 1))
                    sp.wait_ge(s_small, b.ago(2).count(1, 1))
                sp.dma_start(xT_f[:, b.par, :, :], xT[:, :, bass.ds(b.value() * L, L)]).then_inc(s_xT_in[b.par], 16)

            def load_x(b):
                if not b.before(2):
                    sp.wait_ge(s_res, b.ago(2).count(NT, NT))
                sp.dma_start(x_f[:, b.par, :, :], x[bass.ds(b.value() * L, L), :].rearrange("(c p) d -> p c d", p=P)
                             ).then_inc(s_x_in[b.par], 16)

            def store(b):
                sp.wait_ge(s_x1, b.count(NT, NT))
                sp.dma_start(x1[bass.ds(b.value() * L, L), :].rearrange("(c p) d -> p c d", p=P), x1_t[:, b.par, :, :]
                             ).then_inc(s_x1_out[b.par], 16)

            def load_xT_ahead(b):
                if b.value() + 2 < n_seq if b.known() else True:
                    load_xT(b.ago(-2))

            load_xT(Item(0, 0))
            load_xT(Item(0, 1))
            run_steps(sp, n_seq, [(store, 3), (load_xT_ahead, 0), (load_x, 0)], spare=2)
            for par in (0, 1):
                sp.wait_ge(s_x1_out[par], 16 * (n_seq // 2))

        @block.tensor
        def _(pe):
            pe.wait_ge(s_wprep, 3)
            pe.wait_ge(s_load, 16 * N_LOADS)

            def pair(hi, lo, *at):
                return hi[at], lo[at]

            def in_x(b):
                pe.wait_ge(s_xhi, b.count(1, 1))
                pe.wait_ge(s_xlo, b.count(1, 1))
                if b.known() and b.value() == 1:
                    pe.wait_ge(s_tap, 1)
                for m in range(MI):
                    if not b.before(2) and m % 2 == 0:
                        pe.wait_ge(s_t1, b.ago(2).count(NT, m // 2 + 1))
                    for k in range(KD):
                        last = split3(pe, ps_xc[:, m, :],
                                      pair(w_hi, w_lo, slice(None), k, slice(C_X + P * m, C_X + P * m + P)),
                                      pair(xT_hi, xT_lo, slice(None), b.par, k), k == 0, k == KD - 1)
                last.then_inc(s_xc, 1)

            def in_z(b):
                if not b.before(2):
                    pe.wait_ge(s_xt, b.ago(2).count(1, 1))
                elif b.value() == 1:
                    pe.wait_ge(s_zs, 1)
                for c in range(NT):
                    for k in range(KD):
                        last = split3(pe, p45[:, c, :],
                                      pair(xT_hi, xT_lo, slice(None), b.par, k, slice(P * c, P * c + P)),
                                      pair(w_hi, w_lo, slice(None), k, slice(C_Z, C_Z + DI)), k == 0, k == KD - 1)
                last.then_inc(s_z, 1)

            def in_bc(b):
                if not b.before(3):
                    pe.wait_ge(s_res, b.ago(3).count(NT, NT))
                elif not b.before(1):
                    pe.wait_ge(s_bcc, b.ago(1).count(1, 1))
                for w in range(2):
                    for k in range(KD):
                        last = split3(pe, ps_bc[:, w, :],
                                      pair(w_hi, w_lo, slice(None), k, slice(C_BC + P * w, C_BC + P * w + P)),
                                      pair(xT_hi, xT_lo, slice(None), b.par, k), k == 0, k == KD - 1)
                last.then_inc(s_bc, 1)

            def step_size(b):
                if not b.before(2):
                    pe.wait_ge(s_or, b.ago(2).count(1, 1))
                elif b.value() == 1:
                    pe.wait_ge(s_v, 1)
                for c in range(NT):
                    for k in range(KD):
                        last = pe.matmul(ps_dt[:, H * c:H * c + H], xT_f[:, b.par, k, P * c:P * c + P],
                                         w_stage[:, k, C_DT:W_IN], start=(k == 0), stop=(k == KD - 1))
                last.then_inc(s_small, 1)

            def scores(b):
                if b.known() and b.value() == n_seq - 1:
                    pe.wait_ge(s_or, b.ago(1).count(1, 1))
                pe.wait_ge(s_bcc, b.count(1, 1))
                pe.wait_ge(s_l, b.count(1, 1))
                bT, cT = bc[:, b.par, 0, :], bc[:, b.par, 1, :]
                pe.matmul(ps_g[:, 0:2, :].rearrange("p g t -> p (g t)"), bT[:, 0:P], cT, start=True, stop=True)
                pe.matmul(ps_g[:, 2, :], bT[:, P:L], cT[:, P:L], start=True, stop=True)
                pe.matmul(ps_rc[:, 0:H], upto, l_dt[:, b.par, H:2 * H], start=True, stop=True)
                pe.matmul(ps_rc[:, H:2 * H], after, l_dt[:, b.par, 0:H], start=True, stop=True).then_inc(s_g, 1)

            def decay(c):
                def run(b):
                    if c == 0:
                        pe.wait_ge(s_lm, b.count(1, 1))
                        if not b.before(1):
                            pe.wait_ge(s_ylo, b.ago(1).count(1, 1))
                    else:
                        pe.wait_ge(s_exp, b.count(NT, 1))
                    for j in range(2):
                        last = pe.matmul(p23[:, j, :], after,
                                         lm[:, c, 4 * j:4 * j + 4, :].rearrange("p h t -> p (h t)"),
                                         start=True, stop=True)
                    last.then_inc(s_E, 1)
                return run

            def turn_x(b):
                pe.wait_ge(s_sx, b.count(1, 1))
                if b.known() and b.value() == n_seq - 1:
                    pe.wait_ge(s_xt, b.ago(1).count(1, 1))
                else:
                    pe.wait_ge(s_zs, b.ago(-1).count(1, 1))
                for c in range(NT):
                    for m in range(MI):
                        last = pe.transpose(p45[:, c, P * m:P * m + P], sx[:, b.par, m, P * c:P * c + P], ident)
                last.then_inc(s_T, 1)

            def mix(b):
                if b.known() and b.value() == n_seq - 1:
                    pe.wait_ge(s_t1, b.ago(1).count(NT, NT))
                else:
                    pe.wait_ge(s_tap, b.ago(-1).count(1, 1))
                pe.wait_ge(s_xt, b.count(1, 1))
                for c in range(NT):
                    pe.wait_ge(s_mt, b.count(NT, c + 1))
                    for h in range(H):
                        last = pe.matmul(p01[:, c, HD * h:HD * h + HD], mt[:, c, h, :], x_t[:, c, HD * h:HD * h + HD],
                                         start=True, stop=True)
                    last.then_inc(s_Y, 1)

            def mix_off(b):
                pe.wait_ge(s_cx, b.count(1, 1))
                pe.wait_ge(s_rc, b.count(1, 1))
                pe.matmul(p7[:, :], g_m[:, 1, :], cx[:, :], start=True, stop=True).then_inc(s_off, 1)

            def turn_y(b):
                pe.wait_ge(s_y, b.count(NT, NT))
                pe.wait_ge(s_exp, b.count(NT, NT))
                for m in range(MI):
                    for c in range(NT):
                        last = pe.transpose(ps_yT[:, m, P * c:P * c + P], y[:, b.par, c, P * m:P * m + P], ident)
                last.then_inc(s_yT, 1)

            def out(b):
                if b.before(1):
                    pe.wait_ge(s_wout, MI + 2)
                pe.wait_ge(s_ylo, b.count(1, 1))
                if b.known() and b.value() >= n_seq - 2:
                    pe.wait_ge(s_res, b.ago(1).count(NT, NT))
                else:
                    pe.wait_ge(s_bcc, b.ago(-2).count(1, 1))
                for c in range(NT):
                    for m in range(MI):
                        last = split3(pe, ps_out[:, c, :], pair(yT_hi, yT_lo, slice(None), m, slice(P * c, P * c + P)),
                                      pair(wo_hi, wo_lo, slice(None), m), m == 0, m == MI - 1)
                last.then_inc(s_out, 1)

            run_steps(pe, n_seq, [
                (in_x, 0), (in_z, 0), (turn_y, 2), (in_bc, 0), (step_size, 0), (scores, 1), (decay(0), 1), (turn_x, 1),
                (decay(1), 1), (out, 2), (mix, 1), (mix_off, 1)])

        @block.scalar
        def _(act):
            act.wait_ge(s_load, 16 * N_LOADS)
            act.activation(a_neg[:, :], a_neg[:, :], ACT.Exp).then_inc(s_aexp, 1)

            def take_xc(b):
                act.wait_ge(s_xc, b.count(1, 1))
                if b.before(1):
                    act.wait_ge(s_pow, 2)
                else:
                    act.wait_ge(s_conv, b.ago(1).count(12, 12))
                    act.wait_ge(s_sx, b.ago(1).count(1, 1))
                act.activation(xc_pad[:, :, D_CONV - 1:], ps_xc, ACT.Copy).then_inc(s_pad, 1)
                for m in range(MI):
                    last = act.activation(conv[:, m, :], ps_xc[:, m, :], ACT.Identity,
                                          bias=cb[:, m:m + 1], scale=cw[:, m, D_CONV - 1:D_CONV])
                last.then_inc(s_tap, 1)

            def squares(b):
                for c in range(NT):
                    act.wait_ge(s_y, b.count(NT, c + 1))
                    if c:
                        act.wait_ge(s_sq, b.count(NT, c))
                    elif not b.before(1):
                        act.wait_ge(s_sq, b.ago(1).count(NT, NT))
                    if not b.before(2) and c == 0:
                        act.wait_ge(s_ms, b.ago(2).count(1, 1))
                    act.activation(sq[:, :], y[:, b.par, c, :], ACT.Square, accum_out=ss[:, b.par, c:c + 1]
                                   ).then_inc(s_sq, 1)

            def tanh_z(b):
                act.wait_ge(s_z, b.count(1, 1))
                if not b.before(1):
                    act.wait_ge(s_zs, b.ago(1).count(1, 1))
                act.activation(z_t[:, :, :], p45[:, :, :], ACT.Tanh, scale=0.5).then_inc(s_zt, 1)

            def y_high(b):
                act.wait_ge(s_yT, b.count(1, 1))
                if not b.before(1):
                    act.wait_ge(s_out, b.ago(1).count(1, 1))
                act.activation(yT_hi[:, :, :], ps_yT, ACT.Copy).then_inc(s_yhi, 1)

            def take_bc(b):
                act.wait_ge(s_bc, b.count(1, 1))
                if not b.before(2):
                    act.wait_ge(s_g, b.ago(2).count(1, 1))
                act.activation(bc[:, b.par, :, :], ps_bc[0:N_STATE, :, :], ACT.Copy).then_inc(s_bcc, 1)

            def exp_rc(b):
                act.wait_ge(s_g, b.count(1, 1))
                act.wait_ge(s_gm, b.count(1, 1))
                if not b.before(1):
                    act.wait_ge(s_or, b.ago(1).count(1, 1))
                    act.wait_ge(s_cx, b.ago(1).count(1, 1))
                act.activation(rc[:, :], ps_rc, ACT.Exp).then_inc(s_rc, 1)

            def exp_decay(c):
                def run(b):
                    act.wait_ge(s_E, b.count(NT, c + 1))
                    if not b.before(1):
                        act.wait_ge(s_mt, b.ago(1).count(NT, c + 1))
                    act.activation(e_x[:, c, :, :].rearrange("p h t -> p (h t)"),
                                   p23[:, :, :].rearrange("p b t -> p (b t)"), ACT.Exp).then_inc(s_exp, 1)
                return run

            def take_x(b):
                act.wait_ge(s_T, b.count(1, 1))
                if not b.before(1):
                    act.wait_ge(s_Y, b.ago(1).count(NT, NT))
                    act.wait_ge(s_xd, b.ago(1).count(1, 1))
                    act.wait_ge(s_cx, b.ago(1).count(1, 1))
                act.activation(x_t[:, :, :], p45[:, :, :], ACT.Copy).then_inc(s_xt, 1)

            def tanh_conv(b):
                act.wait_ge(s_conv, b.count(12, 12))
                if not b.before(1):
                    act.wait_ge(s_sx, b.ago(1).count(1, 1))
                act.activation(conv_t[:, :, :], conv[:, :, :], ACT.Tanh, scale=0.5).then_inc(s_ct, 1)

            def softplus(b):
                act.wait_ge(s_na, b.count(1, 1))
                act.activation(v_ex[:, :], v_na[:, :], ACT.Exp).then_inc(s_dex, 1)
                act.wait_ge(s_dex, b.count(1, 1))
                if not b.before(1):
                    act.wait_ge(s_sp, b.ago(1).count(1, 1))
                act.activation(v_ln[:, :], v_ex[:, :], ACT.Ln, bias=1.0).then_inc(s_dln, 1)

            run_steps(act, n_seq, [
                (take_xc, 0), (squares, 2), (tanh_z, 0), (y_high, 2), (take_bc, 0), (exp_rc, 1), (exp_decay(0), 1),
                (take_x, 1), (exp_decay(1), 1), (tanh_conv, 0), (softplus, 0)])

        @block.vector
        def _(dve):
            dve.memset(xc_pad[:, :, :], 0.0).then_inc(s_pow, 1)
            dve.memset(pow_half[:, :], -0.5).then_inc(s_pow, 1)
            dve.memset(rms_eps[:, :], 16 * DI * RMS_EPS).then_inc(s_pow, 1)
            dve.memset(ln_eps[:, :], LN_EPS).then_inc(s_pow, 1)
            dve.wait_ge(s_load, 16 * N_LOADS)
            for hi, lo, src in ((w_hi, w_lo, w_stage[:, :, 0:C_DT]),):
                dve.tensor_copy(hi[:, :, :], src).then_inc(s_wprep, 1)
                dve.wait_ge(s_wprep, 1)
                dve.tensor_tensor(lo[:, :, :], src, hi[:, :, :].bitcast(F32), ALU.subtract).then_inc(s_wprep, 1)
            dve.wait_ge(s_aexp, 1)
            dve.tensor_scalar(a_neg[:, :], a_neg[:, :], -1.0, None, ALU.mult).then_inc(s_wprep, 1)

            def prep_out():
                for m in range(MI):
                    dve.tensor_scalar(wo_stage[:, m, :], wo_stage[:, m, :], nw[:, m:m + 1], DI ** 0.5,
                                      ALU.mult, ALU.mult).then_inc(s_wout, 1)
                dve.wait_ge(s_wout, MI)
                dve.tensor_copy(wo_hi[:, :, :], wo_stage[:, :, :]).then_inc(s_wout, 1)
                dve.wait_ge(s_wout, MI + 1)
                dve.tensor_tensor(wo_lo[:, :, :], wo_stage[:, :, :], wo_hi[:, :, :].bitcast(F32), ALU.subtract
                                  ).then_inc(s_wout, 1)

            def x_high(b):
                dve.wait_ge(s_xT_in[b.par], b.half * 16 + 16)
                if not b.before(2):
                    dve.wait_ge(s_bc, b.ago(2).count(1, 1))
                dve.tensor_copy(xT_hi[:, b.par, :, :], xT_f[:, b.par, :, :]).then_inc(s_xhi, 1)

            def taps(b):
                dve.wait_ge(s_tap, b.count(1, 1))
                for k in range(D_CONV - 1):
                    for m in range(MI):
                        if k:
                            dve.wait_ge(s_conv, b.count(12, 4 * (k - 1) + m + 1))
                        dve.scalar_tensor_tensor(out=conv[:, m, :], in0=xc_pad[:, m, k:k + L], scalar=cw[:, m, k:k + 1],
                                                 in1=conv[:, m, :], op0=ALU.mult, op1=ALU.add).then_inc(s_conv, 1)

            def gate(b):
                dve.wait_ge(s_zt, b.count(1, 1))
                if not b.before(2):
                    dve.wait_ge(s_y, b.ago(2).count(NT, NT))
                dve.scalar_tensor_tensor(out=zs[:, b.par, :, :], in0=z_t[:, :, :], scalar=1.0, in1=p45[:, :, :],
                                         op0=ALU.add, op1=ALU.mult).then_inc(s_zs, 1)

            def y_low(b):
                dve.wait_ge(s_yhi, b.count(1, 1))
                dve.tensor_tensor(yT_lo[:, :, :], ps_yT, yT_hi[:, :, :].bitcast(F32), ALU.subtract).then_inc(s_ylo, 1)

            def bias_dt(b):
                dve.wait_ge(s_small, b.count(1, 1))
                if not b.before(1):
                    dve.wait_ge(s_g, b.ago(1).count(1, 1))
                    dve.wait_ge(s_sp, b.ago(1).count(1, 1))
                dve.tensor_tensor(v_dt[:, :].rearrange("p (c h) -> p c h", c=NT),
                                  ps_dt.rearrange("p (c h) -> p c h", c=NT),
                                  dtb[:, :].unsqueeze(1).to_broadcast([P, NT, H]), ALU.add).then_inc(s_v, 1)
                dve.wait_ge(s_v, b.count(1, 1))
                if not b.before(1):
                    dve.wait_ge(s_dex, b.ago(1).count(1, 1))
                dve.scalar_tensor_tensor(out=v_na[:, :], in0=v_dt[:, :], scalar=-1.0, in1=v_dt[:, :],
                                         op0=ALU.mult, op1=ALU.min).then_inc(s_na, 1)

            def mask_g(b):
                dve.wait_ge(s_g, b.count(1, 1))
                if not b.before(1):
                    dve.wait_ge(s_off, b.ago(1).count(1, 1))
                dve.tensor_copy(g_m[:, 1, :], ps_g[:, 1, :])
                dve.tensor_tensor(g_m[:, 0:3:2, :], ps_g[:, 0:3:2, :], upto.unsqueeze(1).to_broadcast([P, 2, P]),
                                  ALU.mult).then_inc(s_gm, 1)

            def weigh(c):
                def run(b):
                    dve.wait_ge(s_exp, b.count(NT, c + 1))
                    dve.wait_ge(s_gm, b.count(1, 1))
                    if not b.before(1):
                        dve.wait_ge(s_Y, b.ago(1).count(NT, c + 1))
                    dve.tensor_tensor(mt[:, c, :, :], e_x[:, c, :, :],
                                      g_m[:, 2 * c, :].unsqueeze(1).to_broadcast([P, H, P]), ALU.mult
                                      ).then_inc(s_mt, 1)
                return run

            def silu_conv(b):
                dve.wait_ge(s_ct, b.count(1, 1))
                if not b.before(2):
                    dve.wait_ge(s_T, b.ago(2).count(1, 1))
                dve.scalar_tensor_tensor(out=sx[:, b.par, :, :], in0=conv_t[:, :, :], scalar=1.0, in1=conv[:, :, :],
                                         op0=ALU.add, op1=ALU.mult).then_inc(s_sx, 1)

            def log_decay(b):
                dve.wait_ge(s_dln, b.count(1, 1))
                dve.scalar_tensor_tensor(out=v_sp[:, :], in0=v_dt[:, :], scalar=0.0, in1=v_ln[:, :],
                                         op0=ALU.max, op1=ALU.add).then_inc(s_sp, 1)
                dve.wait_ge(s_sp, b.count(1, 1))
                if not b.before(2):
                    dve.wait_ge(s_lm, b.ago(2).count(1, 1))
                    dve.wait_ge(s_g, b.ago(2).count(1, 1))
                dve.tensor_tensor(l_dt[:, b.par, :].rearrange("p (c h) -> p c h", c=NT),
                                  v_sp[:, :].rearrange("p (c h) -> p c h", c=NT),
                                  a_neg[:, :].unsqueeze(1).to_broadcast([P, NT, H]), ALU.mult).then_inc(s_l, 1)

            def residual(b):
                dve.wait_ge(s_out, b.count(1, 1))
                dve.wait_ge(s_ri, b.count(1, 1))
                dve.wait_ge(s_x_in[b.par], b.half * 16 + 16)
                if not b.before(1):
                    dve.wait_ge(s_x1, b.ago(1).count(NT, NT))
                for c in range(NT):
                    dve.scalar_tensor_tensor(out=res[:, c, :], in0=ps_out[:, c, :], scalar=rinv[:, b.par, c:c + 1],
                                             in1=x_f[:, b.par, c, :], op0=ALU.mult, op1=ALU.add).then_inc(s_res, 1)
                for c in range(NT):
                    dve.wait_ge(s_res, b.count(NT, c + 1))
                    dve.bn_stats(st[:, c, :], res[:, c, :]).then_inc(s_st, 1)
                free = [] if b.before(1) else [(s_ve, b.ago(1).count(1, 1))]
                wait_apart(dve, spare[0:1, :], (s_st, b.count(NT, NT)), *free)
                for c in range(NT):
                    dve.bn_aggr(mv[:, c, :], st[:, c, :]).then_inc(s_mv, 1)

            def normalise(b):
                dve.wait_ge(s_rs, b.count(1, 1))
                if not b.before(2):
                    dve.wait_ge(s_x1_out[b.par], b.half * 16)
                for c in range(NT):
                    dve.tensor_scalar(x1_t[:, b.par, c, :], res[:, c, :], mv[:, c, 0:1], rstd[:, c:c + 1],
                                      ALU.subtract, ALU.mult).then_inc(s_x1, 1)

            def add_d(b):
                dve.wait_ge(s_xd, b.count(1, 1))
                for c in range(NT):
                    dve.wait_ge(s_Y, b.count(NT, c + 1))
                    if not b.before(1):
                        dve.wait_ge(s_y, b.ago(1).count(NT, NT))
                    dve.tensor_tensor(t1[:, c, :], p01[:, c, :], xd[:, c, :], ALU.add).then_inc(s_t1, 1)
                dve.wait_ge(s_off, b.count(1, 1))
                dve.wait_ge(s_rc, b.count(1, 1))
                if not b.before(1):
                    dve.wait_ge(s_t2, b.ago(1).count(1, 1))
                dve.tensor_tensor(off_r[:, :].rearrange("p (h d) -> p h d", h=H),
                                  p7[:, :].rearrange("p (h d) -> p h d", h=H),
                                  rc[:, 0:H].unsqueeze(2).to_broadcast([P, H, HD]), ALU.mult).then_inc(s_or, 1)

            x_high(Item(0, 0))

            def x_high_next(b):
                if not (b.known() and b.value() + 1 >= n_seq):
                    x_high(b.ago(-1))

            def prep_once(b):
                if b.before(1):
                    prep_out()

            run_steps(dve, n_seq, [
                (prep_once, 0), (x_high_next, 0), (taps, 0), (gate, 0), (y_low, 2), (bias_dt, 0), (mask_g, 1),
                (weigh(0), 1), (weigh(1), 1), (silu_conv, 0), (log_decay, 0), (normalise, 3), (residual, 2),
                (add_d, 1)], spare=2)

        @block.gpsimd
        def _(pool):
            def x_low(b):
                pool.wait_ge(s_xhi, b.count(1, 1))
                if not b.before(2):
                    pool.wait_ge(s_bc, b.ago(2).count(1, 1))
                pool.tensor_tensor(xT_lo[:, b.par, :, :], xT_f[:, b.par, :, :], xT_hi[:, b.par, :, :].bitcast(F32),
                                   ALU.subtract).then_inc(s_xlo, 1)

            def scale_x(b):
                pool.wait_ge(s_xt, b.count(1, 1))
                pool.wait_ge(s_rc, b.count(1, 1))
                if not b.before(1):
                    pool.wait_ge(s_off, b.ago(1).count(1, 1))
                pool.tensor_tensor(cx[:, :].rearrange("p (h d) -> p h d", h=H),
                                   x_t[:, 0, :].rearrange("p (h d) -> p h d", h=H),
                                   rc[:, H:2 * H].unsqueeze(2).to_broadcast([P, H, HD]), ALU.mult).then_inc(s_cx, 1)
                if not b.before(1):
                    pool.wait_ge(s_t1, b.ago(1).count(NT, NT))
                for c in range(NT):
                    last = pool.tensor_tensor(xd[:, c, :].rearrange("p (h d) -> p h d", h=H),
                                              x_t[:, c, :].rearrange("p (h d) -> p h d", h=H),
                                              d_b[:, :].unsqueeze(2).to_broadcast([P, H, HD]), ALU.mult)
                last.then_inc(s_xd, 1)

            def spread_l(b):
                pool.wait_ge(s_l, b.count(1, 1))
                if not b.before(1):
                    pool.wait_ge(s_E, b.ago(1).count(NT, NT))
                for c in range(NT):
                    last = pool.tensor_tensor(lm[:, c, :, :],
                                              l_dt[:, b.par, H * c:H * c + H].unsqueeze(2).to_broadcast([P, H, P]),
                                              upto.unsqueeze(1).to_broadcast([P, H, P]), ALU.mult)
                last.then_inc(s_lm, 1)

            def join(b):
                pool.wait_ge(s_t1, b.count(NT, 1))
                if not b.before(2):
                    pool.wait_ge(s_yT, b.ago(2).count(1, 1))
                    pool.wait_ge(s_sq, b.ago(2).count(NT, NT))
                pool.wait_ge(s_zs, b.count(1, 1))
                pool.tensor_tensor(y[:, b.par, 0, :], t1[:, 0, :], zs[:, b.par, 0, :], ALU.mult).then_inc(s_y, 1)
                pool.wait_ge(s_or, b.count(1, 1))
                if not b.before(1):
                    pool.wait_ge(s_y, b.ago(1).count(NT, NT))
                pool.tensor_tensor(t2[:, :], t1[:, 1, :], off_r[:, :], ALU.add).then_inc(s_t2, 1)
                pool.wait_ge(s_t2, b.count(1, 1))
                pool.tensor_tensor(y[:, b.par, 1, :], t2[:, :], zs[:, b.par, 1, :], ALU.mult).then_inc(s_y, 1)

            def inv_rms(b):
                pool.wait_ge(s_sq, b.count(NT, NT))
                if not b.before(1):
                    pool.wait_ge(s_ri, b.ago(1).count(1, 1))
                pool.tensor_tensor(ms[:, :], ss[:, b.par, :], rms_eps[:, :], ALU.add).then_inc(s_ms, 1)
                pool.wait_ge(s_ms, b.count(1, 1))
                if not b.before(2):
                    pool.wait_ge(s_res, b.ago(2).count(NT, NT))
                pool.tensor_tensor(rinv[:, b.par, :], ms[:, :], pow_half[:, 0:NT], ALU.pow).then_inc(s_ri, 1)

            def inv_std(b):
                pool.wait_ge(s_mv, b.count(NT, NT))
                if not b.before(1):
                    pool.wait_ge(s_rs, b.ago(1).count(1, 1))
                pool.tensor_tensor(ve[:, :], mv[:, :, 1], ln_eps[:, :], ALU.add).then_inc(s_ve, 1)
                pool.wait_ge(s_ve, b.count(1, 1))
                if not b.before(1):
                    pool.wait_ge(s_x1, b.ago(1).count(NT, NT))
                pool.tensor_tensor(rstd[:, :], ve[:, :], pow_half[:, 0:NT], ALU.pow).then_inc(s_rs, 1)

            pool.wait_ge(s_load, 16 * N_LOADS)
            pool.wait_ge(s_pow, 4)
            x_low(Item(0, 0))

            def x_low_next(b):
                if not (b.known() and b.value() + 1 >= n_seq):
                    x_low(b.ago(-1))

            run_steps(pool, n_seq, [
                (x_low_next, 0), (inv_rms, 2), (scale_x, 1), (spread_l, 0), (join, 1), (inv_std, 2)], spare=2)


class Unit:
    PER = 8

    def __init__(self, item, v):
        self.item, self.v, self.par = item, v, v % 2

    def ago(self, n):
        back = -((self.v - n) // self.PER)
        return Unit(self.item.ago(back), (self.v - n) % self.PER)

    def before(self, n):
        return self.item.known() and self.item.value() * self.PER + self.v < n

    def count(self, per, done):
        return self.item.count(self.PER * per, self.v * per + done)


def by_unit(stages, after):
    out = []
    for v in range(Unit.PER):
        for stage, ulag, lag in stages:
            back = -((v - ulag) // Unit.PER)

            def run(b, stage=stage, w=(v - ulag) % Unit.PER):
                stage(Unit(b, w))
            out.append((run, lag + back))
        out += after.get(v, [])
    return out


def attention_phase(nc, n_seq, x1, ctxT, x2, wq, bq, wk, bk, wv, bv, wo, bo, masks):
    LK, H, HD = 77, 16, 64
    DH = H * HD
    MH = DH // P
    G = 4
    GM = G * HD // P
    LN_EPS = 1e-5

    with ExitStack() as ctx:
        def sb(name, shape, dt=F32):
            return ctx.enter_context(nc.sbuf_tensor("b_" + name, shape, dt))

        def sem(name):
            return ctx.enter_context(nc.semaphore("b_" + name))

        w_stage = sb("w_stage", [P, 3, MH * D])
        wq_hi = sb("wq_hi", [P, KD, DH], F32R)
        wq_lo = sb("wq_lo", [P, KD, DH], F32R)
        wv_hi = sb("wv_hi", [P, KD, DH], F32R)
        wv_lo = sb("wv_lo", [P, KD, DH], F32R)
        wo_hi = sb("wo_hi", [P, MH, D], F32R)
        wo_lo = sb("wo_lo", [P, MH, D], F32R)
        wk_f = sb("wk_f", [P, KD, DH])
        bq_c = sb("bq_c", [P, MH])
        bk_c = sb("bk_c", [P, MH])
        bv_b = sb("bv_b", [P, DH])
        bo_b = sb("bo_b", [P, D])
        mk = sb("mk", [P, 3, P])
        ident = mk[:, 2, :]
        spare = sb("spare", [P, 1])
        pow_half = sb("pow_half", [P, 1])
        ln_eps = sb("ln_eps", [P, 1])

        xa = sb("xa", [P, 2, NT, D])
        xr = sb("xr", [P, 2, NT, D])
        xrb = sb("xrb", [P, 2, NT, D])
        xT_hi = sb("xT_hi", [P, 2, KD, L], F32R)
        xT_lo = sb("xT_lo", [P, 2, KD, L], F32R)
        c_f = sb("c_f", [P, 2, KD, LK])
        c_hi = sb("c_hi", [P, 2, KD, LK], F32R)
        c_lo = sb("c_lo", [P, 2, KD, LK], F32R)
        qT = sb("qT", [P, 2, MH, L])
        kz = sb("kz", [P, 2, MH, 2, LK])
        vv = sb("vv", [LK, 2, H, HD + 1])
        mx = sb("mx", [P, 2, G])
        sd = sb("sd", [P, 2, G, LK])
        pe_ = sb("pe_", [P, 2, G, LK])
        pT = sb("pT", [LK, 2, G, P])
        rec = sb("rec", [P, 2, G])
        o_n = sb("o_n", [P, 2, G, HD])
        oT_hi = sb("oT_hi", [P, 2, GM, P], F32R)
        oT_lo = sb("oT_lo", [P, 2, GM, P], F32R)
        res = sb("res", [P, 2, D])
        st = sb("st", [P, 2, 6])
        mv = sb("mv", [P, 2, 2])
        ve = sb("ve", [P, 2])
        rstd = sb("rstd", [P, 2])
        x2_t = sb("x2_t", [P, 2, NT, D])

        ps_s = [ctx.enter_context(nc.psum_tensor(f"b_ps_s{i}", [P, 512], F32)) for i in range(2)]
        ps_qk = ctx.enter_context(nc.psum_tensor("b_ps_qk", [P, 512], F32))
        ps_x = ctx.enter_context(nc.psum_tensor("b_ps_x", [P, 512], F32))
        ps_pT = ctx.enter_context(nc.psum_tensor("b_ps_pT", [P, 512], F32))
        ps_o = ctx.enter_context(nc.psum_tensor("b_ps_o", [P, 512], F32))
        ps_oT = ctx.enter_context(nc.psum_tensor("b_ps_oT", [P, 512], F32))
        ps_out = ctx.enter_context(nc.psum_tensor("b_ps_out", [P, 512], F32))

        s_w1, s_w2, s_w3, s_c = sem("w1"), sem("w2"), sem("w3"), sem("const")
        s_prep, s_zero = sem("prep"), sem("zero")
        s_xa_in, s_xr_in, s_c_in, s_x2_out = ([sem(f"{n}{i}") for i in range(2)]
                                              for n in ("xa_in", "xr_in", "c_in", "x2_out"))
        s_x, s_qk, s_v, s_s, s_pT, s_o, s_oT, s_out = (
            sem(n) for n in ("x", "qk", "v", "s", "pT", "o", "oT", "out"))
        s_xhi, s_qkc, s_exp, s_ohi = (sem(n) for n in ("xhi", "qkc", "exp", "ohi"))
        s_pTc = [sem("pTc0"), sem("pTc1")]
        s_xlo, s_chi, s_vc, s_mx, s_sd, s_rec, s_on, s_olo, s_res, s_st, s_mv, s_x2 = (
            sem(n) for n in ("xlo", "chi", "vc", "mx", "sd", "rec", "on", "olo", "res", "st", "mv", "x2"))
        s_clo, s_xrb, s_ve, s_rs = (sem(n) for n in ("clo", "xrb", "ve", "rs"))

        block = ctx.enter_context(nc.Block())

        def half_count(u):
            return u.item.count(4, u.v // 2 + 1)

        def copy_p(eng, u):
            eng.wait_ge(s_pT, u.count(1, 1))
            if not u.before(2):
                eng.wait_ge(s_o, u.ago(2).count(1, 1))

        @block.sync
        def _(sp):
            sp.dma_start(w_stage[:, 0, :].rearrange("p (k n) -> p k n", k=KD), wq.rearrange("(k p) n -> p k n", p=P)
                         ).then_inc(s_w1, 16)
            sp.dma_start(w_stage[:, 1, :].rearrange("p (k n) -> p k n", k=KD), wv.rearrange("(k p) n -> p k n", p=P)
                         ).then_inc(s_w2, 16)
            sp.dma_start(w_stage[:, 2, :].rearrange("p (k n) -> p k n", k=MH), wo.rearrange("(k p) n -> p k n", p=P)
                         ).then_inc(s_w3, 16)
            sp.dma_start(wk_f[:, :, :], wk.rearrange("(k p) n -> p k n", p=P)).then_inc(s_c, 16)
            sp.dma_start(bq_c[:, :], bq).then_inc(s_c, 16)
            sp.dma_start(bk_c[:, :], bk).then_inc(s_c, 16)
            sp.dma_start(bv_b[:, :], bv.partition_broadcast(P)).then_inc(s_c, 16)
            sp.dma_start(bo_b[:, :], bo.partition_broadcast(P)).then_inc(s_c, 16)
            sp.dma_start(mk[:, :, :], masks).then_inc(s_c, 16)

            def rows(a, b):
                return a[bass.ds(b.value() * L, L), :].rearrange("(c p) d -> p c d", p=P)

            def load_xa(b):
                if not b.before(2):
                    sp.wait_ge(s_x, b.ago(2).count(1, 1))
                sp.dma_start(xa[:, b.par, :, :], rows(x1, b)).then_inc(s_xa_in[b.par], 16)

            def load_c(b):
                if not b.before(2):
                    sp.wait_ge(s_qk, b.ago(2).count(8, 8))
                    sp.wait_ge(s_clo, b.ago(2).count(1, 1))
                sp.dma_start(c_f[:, b.par, :, :], ctxT[:, :, bass.ds(b.value() * LK, LK)]).then_inc(s_c_in[b.par], 16)

            def load_xr(b):
                if not b.before(2):
                    sp.wait_ge(s_xrb, b.ago(2).count(1, 1))
                sp.dma_start(xr[:, b.par, :, :], rows(x1, b)).then_inc(s_xr_in[b.par], 16)

            def store(b):
                sp.wait_ge(s_x2, b.count(NT, NT))
                sp.dma_start(rows(x2, b), x2_t[:, b.par, :, :]).then_inc(s_x2_out[b.par], 16)

            def load_xa_ahead(b):
                if not (b.known() and b.value() + 1 >= n_seq):
                    load_xa(b.ago(-1))

            load_xa(Item(0, 0))
            run_steps(sp, n_seq, [(load_c, 0), (load_xa_ahead, 0), (load_xr, 1), (store, 3)], spare=2)
            for par in (0, 1):
                sp.wait_ge(s_x2_out[par], 16 * (n_seq // 2))

        @block.tensor
        def _(pe):
            pe.wait_ge(s_c, 16 * 6)
            pe.wait_ge(s_prep, 6)

            def turn_x(b):
                pe.wait_ge(s_xa_in[b.par], b.half * 16 + 16)
                if not b.before(1):
                    pe.wait_ge(s_vc, b.ago(1).count(2, 2))
                for k in range(KD):
                    for c in range(NT):
                        last = pe.transpose(ps_x[:, L * k + P * c:L * k + P * c + P],
                                            xa[:, b.par, c, P * k:P * k + P], ident)
                last.then_inc(s_x, 1)

            def queries_keys(u):
                b, m = u.item, u.v
                if m == 0:
                    pe.wait_ge(s_xhi, b.count(1, 1))
                    pe.wait_ge(s_xlo, b.count(1, 1))
                    pe.wait_ge(s_c_in[b.par], b.half * 16 + 16)
                if not u.before(1):
                    pe.wait_ge(s_qkc, u.ago(1).count(1, 1))
                for k in range(KD):
                    split3(pe, ps_qk[:, 0:L], (wq_hi[:, k, P * m:P * m + P], wq_lo[:, k, P * m:P * m + P]),
                           (xT_hi[:, b.par, k, :], xT_lo[:, b.par, k, :]), k == 0, k == KD - 1)
                for k in range(KD):
                    last = pe.matmul(ps_qk[:, L:L + LK], wk_f[:, k, P * m:P * m + P], c_f[:, b.par, k, :],
                                     start=(k == 0), stop=(k == KD - 1))
                last.then_inc(s_qk, 1)

            def values(half):
                def run(b):
                    pe.wait_ge(s_clo, b.count(1, 1))
                    if half:
                        pe.wait_ge(s_vc, b.count(2, 1))
                    else:
                        pe.wait_ge(s_xlo, b.count(1, 1))
                    for k in range(KD):
                        last = split3(pe, ps_x[0:LK, :], (c_hi[:, b.par, k, :], c_lo[:, b.par, k, :]),
                                      (wv_hi[:, k, 512 * half:512 * half + 512],
                                       wv_lo[:, k, 512 * half:512 * half + 512]), k == 0, k == KD - 1)
                    last.then_inc(s_v, 1)
                return run

            def scores(u):
                b, j, g = u.item, u.v // 4, u.v % 4
                pe.wait_ge(s_qkc, b.count(8, 8))
                if not u.before(2):
                    pe.wait_ge(s_sd, u.ago(2).count(1, 1))
                for i in range(GM):
                    last = pe.matmul(ps_s[u.par][:, 2 * LK * i:2 * LK * i + 2 * LK],
                                     qT[:, b.par, GM * g + i, P * j:P * j + P],
                                     kz[:, b.par, GM * g + i, :, :].rearrange("p a k -> p (a k)"),
                                     start=True, stop=True)
                last.then_inc(s_s, 1)

            def turn_p(u):
                pe.wait_ge(s_exp, u.count(1, 1))
                if not u.before(1):
                    prev = u.ago(1)
                    pe.wait_ge(s_pTc[prev.par], half_count(prev))
                for i in range(G):
                    last = pe.transpose(ps_pT[0:LK, P * i:P * i + P], pe_[:, u.par, i, :], ident)
                last.then_inc(s_pT, 1)

            def attend(u):
                b, g = u.item, u.v % 4
                pe.wait_ge(s_pTc[u.par], half_count(u))
                pe.wait_ge(s_vc, b.count(2, 2))
                if not u.before(1):
                    pe.wait_ge(s_on, u.ago(1).count(1, 1))
                for i in range(G):
                    last = pe.matmul(ps_o[:, (HD + 1) * i:(HD + 1) * i + HD + 1], pT[:, u.par, i, :],
                                     vv[:, b.par, G * g + i, :], start=True, stop=True)
                last.then_inc(s_o, 1)

            def turn_o(u):
                pe.wait_ge(s_on, u.count(1, 1))
                if not u.before(1):
                    pe.wait_ge(s_olo, u.ago(1).count(1, 1))
                flat = o_n[:, u.par, :, :].rearrange("p g d -> p (g d)")
                for i in range(GM):
                    last = pe.transpose(ps_oT[:, P * i:P * i + P], flat[:, P * i:P * i + P], ident)
                last.then_inc(s_oT, 1)

            def project(u):
                b, j, g = u.item, u.v // 4, u.v % 4
                pe.wait_ge(s_olo, u.count(1, 1))
                if g == 0 and not u.before(4):
                    pe.wait_ge(s_res, u.ago(4).item.count(NT, u.ago(4).v // 4 + 1))
                for i in range(GM):
                    last = split3(pe, ps_out[:, 0:D], (oT_hi[:, u.par, i, :], oT_lo[:, u.par, i, :]),
                                  (wo_hi[:, GM * g + i, :], wo_lo[:, GM * g + i, :]),
                                  g == 0 and i == 0, g == 3 and i == GM - 1)
                last.then_inc(s_out, 1)

            run_steps(pe, n_seq, by_unit(
                [(queries_keys, 0, 1), (scores, 0, 2), (turn_p, 1, 2), (attend, 2, 2), (turn_o, 3, 2), (project, 4, 2)],
                {0: [(values(0), 1)], 2: [(values(1), 1)], 5: [(turn_x, 0)]}))

        @block.scalar
        def _(act):
            act.wait_ge(s_c, 16 * 6)
            act.wait_ge(s_zero, 3)

            def x_high(b):
                act.wait_ge(s_x, b.count(1, 1))
                if not b.before(2):
                    act.wait_ge(s_qk, b.ago(2).count(8, 8))
                act.activation(xT_hi[:, b.par, :, :].rearrange("p k t -> p (k t)"), ps_x[:, :], ACT.Copy
                               ).then_inc(s_xhi, 1)

            def copy_qk(u):
                b, m = u.item, u.v
                act.wait_ge(s_qk, u.count(1, 1))
                if m == 0 and not b.before(2):
                    act.wait_ge(s_s, b.ago(2).count(8, 8))
                act.activation(qT[:, b.par, m, :], ps_qk[:, 0:L], ACT.Identity, bias=bq_c[:, m:m + 1])
                for i in range(2):
                    half = slice(HD * i, HD * i + HD)
                    last = act.activation(kz[half, b.par, m, i, :], ps_qk[half, L:L + LK], ACT.Identity,
                                          bias=bk_c[half, m:m + 1])
                last.then_inc(s_qkc, 1)

            def exps(u):
                act.wait_ge(s_sd, u.count(1, 1))
                if not u.before(2):
                    act.wait_ge(s_pT, u.ago(2).count(1, 1))
                act.activation(pe_[:, u.par, :, :], sd[:, u.par, :, :], ACT.Exp, scale=HD ** -0.5).then_inc(s_exp, 1)

            def copy_p_odd(u):
                if u.par == 1:
                    copy_p(act, u)
                    act.activation(pT[:, u.par, :, :].rearrange("p g q -> p (g q)"), ps_pT[0:LK, :], ACT.Copy
                                   ).then_inc(s_pTc[1], 1)

            def o_high(u):
                act.wait_ge(s_oT, u.count(1, 1))
                if not u.before(2):
                    act.wait_ge(s_out, u.ago(2).count(1, 1))
                act.activation(oT_hi[:, u.par, :, :].rearrange("p i q -> p (i q)"), ps_oT[:, 0:GM * P], ACT.Copy
                               ).then_inc(s_ohi, 1)

            run_steps(act, n_seq, by_unit(
                [(copy_qk, 0, 1), (copy_p_odd, 1, 2), (exps, 0, 2), (o_high, 3, 2)], {5: [(x_high, 0)]}))

        @block.vector
        def _(dve):
            dve.memset(kz[:, :, :, :, :], 0.0).then_inc(s_zero, 1)
            dve.memset(vv[:, :, :, :], 1.0).then_inc(s_zero, 1)
            dve.memset(pow_half[:, :], -0.5).then_inc(s_zero, 1)
            dve.memset(ln_eps[:, :], LN_EPS).then_inc(s_zero, 1)
            for n, (s_w, hi, lo) in enumerate(((s_w1, wq_hi, wq_lo), (s_w2, wv_hi, wv_lo), (s_w3, wo_hi, wo_lo))):
                dve.wait_ge(s_w, 16)
                src = w_stage[:, n, :].rearrange("p (k n) -> p k n", k=hi.shape[1])
                dve.tensor_copy(hi[:, :, :], src).then_inc(s_prep, 1)
                dve.wait_ge(s_prep, 2 * n + 1)
                dve.tensor_tensor(lo[:, :, :], src, hi[:, :, :].bitcast(F32), ALU.subtract).then_inc(s_prep, 1)
            dve.wait_ge(s_c, 16 * 6)
            dve.wait_ge(s_zero, 3)

            def x_low(b):
                dve.wait_ge(s_xhi, b.count(1, 1))
                dve.tensor_tensor(xT_lo[:, b.par, :, :].rearrange("p k t -> p (k t)"), ps_x[:, :],
                                  xT_hi[:, b.par, :, :].rearrange("p k t -> p (k t)").bitcast(F32), ALU.subtract
                                  ).then_inc(s_xlo, 1)

            def c_high(b):
                dve.wait_ge(s_c_in[b.par], b.half * 16 + 16)
                if not b.before(2):
                    dve.wait_ge(s_v, b.ago(2).count(2, 2))
                dve.tensor_copy(c_hi[:, b.par, :, :], c_f[:, b.par, :, :]).then_inc(s_chi, 1)

            def copy_v(half):
                def run(b):
                    dve.wait_ge(s_v, b.count(2, half + 1))
                    if not b.before(2):
                        dve.wait_ge(s_o, b.ago(2).count(8, 8))
                    dve.tensor_tensor(vv[:, b.par, 8 * half:8 * half + 8, 0:HD],
                                      ps_x[0:LK, :].rearrange("p (h d) -> p h d", h=8),
                                      bv_b[0:LK, 512 * half:512 * half + 512].rearrange("p (h d) -> p h d", h=8),
                                      ALU.add).then_inc(s_vc, 1)
                return run

            def subtract_max(u):
                dve.wait_ge(s_s, u.count(1, 1))
                s = ps_s[u.par][:, 0:G * LK].rearrange("p (g k) -> p g k", g=G)
                dve.tensor_reduce(mx[:, u.par, :], s, AX.X, ALU.max).then_inc(s_mx, 1)
                dve.wait_ge(s_mx, u.count(1, 1))
                if not u.before(2):
                    dve.wait_ge(s_exp, u.ago(2).count(1, 1))
                dve.tensor_tensor(sd[:, u.par, :, :], s, mx[:, u.par, :].unsqueeze(2).to_broadcast([P, G, LK]),
                                  ALU.subtract).then_inc(s_sd, 1)

            def copy_p_even(u):
                if u.par == 0:
                    copy_p(dve, u)
                    dve.tensor_copy(pT[:, u.par, :, :].rearrange("p g q -> p (g q)"), ps_pT[0:LK, :]
                                    ).then_inc(s_pTc[0], 1)

            def divide(u):
                dve.wait_ge(s_o, u.count(1, 1))
                o = ps_o[:, 0:G * (HD + 1)].rearrange("p (g d) -> p g d", g=G)
                dve.reciprocal(rec[:, u.par, :], o[:, :, HD]).then_inc(s_rec, 1)
                dve.wait_ge(s_rec, u.count(1, 1))
                if not u.before(2):
                    dve.wait_ge(s_oT, u.ago(2).count(1, 1))
                dve.tensor_tensor(o_n[:, u.par, :, :], o[:, :, 0:HD],
                                  rec[:, u.par, :].unsqueeze(2).to_broadcast([P, G, HD]), ALU.mult).then_inc(s_on, 1)

            def o_low(u):
                dve.wait_ge(s_ohi, u.count(1, 1))
                dve.tensor_tensor(oT_lo[:, u.par, :, :].rearrange("p i q -> p (i q)"), ps_oT[:, 0:GM * P],
                                  oT_hi[:, u.par, :, :].rearrange("p i q -> p (i q)").bitcast(F32), ALU.subtract
                                  ).then_inc(s_olo, 1)

            def residual(u):
                if u.v % 4 != 3:
                    return
                b, j = u.item, u.v // 4
                dve.wait_ge(s_out, u.count(1, 1))
                if j == 0:
                    dve.wait_ge(s_xrb, b.count(1, 1))
                if not b.before(1):
                    dve.wait_ge(s_x2, b.ago(1).count(NT, j + 1))
                dve.tensor_tensor(res[:, j, :], ps_out[:, 0:D], xrb[:, b.par, j, :], ALU.add).then_inc(s_res, 1)
                dve.wait_ge(s_res, b.count(NT, j + 1))
                dve.bn_stats(st[:, j, :], res[:, j, :]).then_inc(s_st, 1)
                wait_apart(dve, spare[0:1, :], (s_st, b.count(NT, j + 1)))
                dve.bn_aggr(mv[:, j, :], st[:, j, :]).then_inc(s_mv, 1)

            def normalise(u):
                if u.v % 4 != 3:
                    return
                b, j = u.item, u.v // 4
                dve.wait_ge(s_rs, b.count(NT, j + 1))
                if not b.before(2):
                    dve.wait_ge(s_x2_out[b.par], b.half * 16)
                dve.tensor_scalar(x2_t[:, b.par, j, :], res[:, j, :], mv[:, j, 0:1], rstd[:, j:j + 1],
                                  ALU.subtract, ALU.mult).then_inc(s_x2, 1)

            run_steps(dve, n_seq, by_unit(
                [(subtract_max, 0, 2), (copy_p_even, 1, 2), (divide, 2, 2), (o_low, 3, 2), (residual, 4, 2),
                 (normalise, 5, 2)],
                {0: [(copy_v(0), 1)], 2: [(copy_v(1), 1)], 5: [(x_low, 0), (c_high, 0)]}))

        @block.gpsimd
        def _(pool):
            pool.wait_ge(s_c, 16 * 6)
            pool.wait_ge(s_zero, 4)

            def c_low(b):
                pool.wait_ge(s_chi, b.count(1, 1))
                if not b.before(2):
                    pool.wait_ge(s_v, b.ago(2).count(2, 2))
                pool.tensor_tensor(c_lo[:, b.par, :, :], c_f[:, b.par, :, :], c_hi[:, b.par, :, :].bitcast(F32),
                                   ALU.subtract).then_inc(s_clo, 1)

            def add_bo(b):
                pool.wait_ge(s_xr_in[b.par], b.half * 16 + 16)
                if not b.before(2):
                    pool.wait_ge(s_res, b.ago(2).count(NT, NT))
                pool.tensor_tensor(xrb[:, b.par, :, :], xr[:, b.par, :, :],
                                   bo_b[:, :].unsqueeze(1).to_broadcast([P, NT, D]), ALU.add).then_inc(s_xrb, 1)

            def inv_std(u):
                if u.v % 4 != 3:
                    return
                b, j = u.item, u.v // 4
                pool.wait_ge(s_mv, b.count(NT, j + 1))
                pool.tensor_tensor(ve[:, j:j + 1], mv[:, j, 1:2], ln_eps[:, :], ALU.add).then_inc(s_ve, 1)
                pool.wait_ge(s_ve, b.count(NT, j + 1))
                if not b.before(1):
                    pool.wait_ge(s_x2, b.ago(1).count(NT, j + 1))
                pool.tensor_tensor(rstd[:, j:j + 1], ve[:, j:j + 1], pow_half[:, :], ALU.pow).then_inc(s_rs, 1)

            run_steps(pool, n_seq, by_unit([(inv_std, 4, 2)], {5: [(c_low, 0), (add_bo, 1)]}))


def experts_phase(nc, n_seq, x2, out, gate_w, w1, b1, w2, b2, ln_g, ln_b, masks):
    E, F = 8, 512
    MF = F // P
    LN_E, LN_EPS = 1e-6, 1e-5
    assert E == Unit.PER

    with ExitStack() as ctx:
        def sb(name, shape, dt=F32):
            return ctx.enter_context(nc.sbuf_tensor("c_" + name, shape, dt))

        def sem(name):
            return ctx.enter_context(nc.semaphore("c_" + name))

        stage = sb("stage", [P, 2, 2 * F])
        w1_hi = sb("w1_hi", [P, E, KD, F], F32R)
        w1_lo = sb("w1_lo", [P, E, KD, F], F32R)
        w2_hi = sb("w2_hi", [P, E, MF, D], F32R)
        w2_lo = sb("w2_lo", [P, E, MF, D], F32R)
        gw = sb("gw", [P, KD, E])
        b1_c = sb("b1_c", [P, E, MF])
        b2_b = sb("b2_b", [P, E, D])
        g_b = sb("g_b", [P, E, D])
        lnb = sb("lnb", [E, D])
        ident = sb("ident", [P, P])
        spare = sb("spare", [P, 1])
        pow_half = sb("pow_half", [P, NT])
        ln_e_eps = sb("ln_e_eps", [P, NT])
        ln_eps = sb("ln_eps", [P, NT])
        iota_e = sb("iota_e", [P, E])

        xa = sb("xa", [P, 2, NT, D])
        xT_f = sb("xT_f", [P, KD, L])
        xT_hi = sb("xT_hi", [P, 2, KD, L], F32R)
        xT_lo = sb("xT_lo", [P, 2, KD, L], F32R)
        hid = sb("hid", [P, MF * L])
        h_hi = sb("h_hi", [P, 2, MF * L], F32R)
        h_lo = sb("h_lo", [P, 2, MF * L], F32R)
        sg = sb("sg", [P, NT, E])
        top = sb("top", [P, NT, 8])
        idx = sb("idx", [P, NT, 8], U32)
        idx_f = sb("idx_f", [P, NT, 2])
        gap = sb("gap", [P, NT])
        e2 = sb("e2", [P, NT])
        e2p = sb("e2p", [P, NT])
        wt = sb("wt", [P, NT, 2])
        pick = sb("pick", [P, NT, 2, E])
        wE = sb("wE", [P, 2, NT, E])
        wET = sb("wET", [E, L])
        xb = sb("xb", [P, 2, NT, D])
        yy = sb("yy", [P, NT, D])
        st = sb("st", [P, NT, 6])
        mv = sb("mv", [P, 2, NT, 2])
        ve = sb("ve", [P, NT])
        rs = sb("rs", [P, NT])
        sc = sb("sc", [P, 2, NT])
        tt = sb("tt", [P, 2, NT, D])
        acc = sb("acc", [P, 2, NT, D])
        fst = sb("fst", [P, NT, 6])
        fmv = sb("fmv", [P, NT, 2])
        fve = sb("fve", [P, NT])
        frs = sb("frs", [P, NT])
        o_t = sb("o_t", [P, NT, D])

        ps_h = [ctx.enter_context(nc.psum_tensor(f"c_ps_h{i}", [P, 2, 512], F32)) for i in range(2)]
        ps_o = [ctx.enter_context(nc.psum_tensor(f"c_ps_o{i}", [P, 512], F32)) for i in range(2)]
        ps_x = ctx.enter_context(nc.psum_tensor("c_ps_x", [P, 512], F32))
        ps_g = ctx.enter_context(nc.psum_tensor("c_ps_g", [P, 512], F32))

        s_w = [sem(f"w{j}") for j in range(2)]
        s_c, s_one = sem("const"), sem("one")
        s_wh, s_wl = sem("wh"), sem("wl")
        s_xa_in = [sem(f"xa_in{i}") for i in range(2)]
        s_o_out = sem("o_out")
        s_x, s_g, s_wt, s_wb, s_h, s_o = (sem(n) for n in ("x", "g", "wt", "wb", "h", "o"))
        s_xf, s_e2, s_gelu, s_hhi, s_wtc = (sem(n) for n in ("xf", "e2", "gelu", "hhi", "wtc"))
        s_xhi, s_sg, s_top, s_idx, s_if, s_gap, s_p1, s_r, s_w2, s_pick, s_wE = (
            sem(n) for n in ("xhi", "sg", "top", "idx", "if", "gap", "p1", "r", "w2", "pick", "wE"))
        s_hlo, s_y, s_st, s_mv, s_t, s_a0, s_acc, s_fst, s_fmv, s_fo = (
            sem(n) for n in ("hlo", "y", "st", "mv", "t", "a0", "acc", "fst", "fmv", "fo"))
        s_xlo, s_xb, s_ve, s_rs, s_sc, s_fve, s_frs = (
            sem(n) for n in ("xlo", "xb", "ve", "rs", "sc", "fve", "frs"))

        block = ctx.enter_context(nc.Block())

        def rows(a, b):
            return a[bass.ds(b.value() * L, L), :].rearrange("(c p) d -> p c d", p=P)

        @block.sync
        def _(sp):
            sp.dma_start(ident[:, :], masks[:, 2, :]).then_inc(s_c, 16)
            sp.dma_start(gw[:, :, :], gate_w.rearrange("(k p) e -> p k e", p=P)).then_inc(s_c, 16)
            sp.dma_start(xa[:, 0, :, :], rows(x2, Item(0, 0))).then_inc(s_xa_in[0], 16)
            sp.dma_start(b1_c[:, :, :], b1).then_inc(s_c, 16)
            sp.dma_start(lnb[:, :], ln_b).then_inc(s_c, 16)
            sp.dma_start(b2_b[:, :, :], b2.partition_broadcast(P)).then_inc(s_c, 16)
            sp.dma_start(g_b[:, :, :], ln_g.partition_broadcast(P)).then_inc(s_c, 16)
            for e in range(E):
                for j, (w, s_split) in enumerate(((w1, s_wh), (w2, s_wl))):
                    if e >= 1:
                        sp.wait_ge(s_split, 2 * e)
                    k = KD if j == 0 else MF
                    sp.dma_start(stage[:, j, :].rearrange("p (k n) -> p k n", k=k),
                                 w[e].rearrange("(k p) n -> p k n", p=P)).then_inc(s_w[j], 16)

            def load(b):
                if not b.before(2):
                    sp.wait_ge(s_xb, b.ago(2).count(E, E))
                sp.dma_start(xa[:, b.par, :, :], rows(x2, b)).then_inc(s_xa_in[b.par], 16)

            def load_ahead(b):
                if not (b.known() and b.value() + 1 >= n_seq):
                    load(b.ago(-1))

            def store(b):
                sp.wait_ge(s_fo, b.count(NT, NT))
                sp.dma_start(rows(out, b), o_t[:, :, :]).then_inc(s_o_out, 16)

            run_steps(sp, n_seq, [(load_ahead, 1), (store, 2)])
            sp.wait_ge(s_o_out, 16 * n_seq)

        @block.tensor
        def _(pe):
            pe.wait_ge(s_c, 16 * 6)

            def turn_x(b):
                pe.wait_ge(s_xa_in[b.par], b.half * 16 + 16)
                if not b.before(1):
                    pe.wait_ge(s_xhi, b.ago(1).count(1, 1))
                for k in range(KD):
                    for c in range(NT):
                        last = pe.transpose(ps_x[:, L * k + P * c:L * k + P * c + P],
                                            xa[:, b.par, c, P * k:P * k + P], ident[:, :])
                last.then_inc(s_x, 1)

            def gate(b):
                pe.wait_ge(s_xf, b.count(1, 1))
                if not b.before(1):
                    pe.wait_ge(s_a0, b.ago(1).count(NT, NT))
                for c in range(NT):
                    for k in range(KD):
                        last = pe.matmul(ps_g[:, E * c:E * c + E], xT_f[:, k, P * c:P * c + P], gw[:, k, :],
                                         start=(k == 0), stop=(k == KD - 1))
                last.then_inc(s_g, 1)

            def turn_w(b):
                pe.wait_ge(s_wE, b.count(1, 1))
                for c in range(NT):
                    last = pe.transpose(ps_g[0:E, P * c:P * c + P], wE[:, b.par, c, :], ident[:, :])
                last.then_inc(s_wt, 1)

            def bias_w(b):
                pe.wait_ge(s_wtc, b.count(1, 1))
                for c in range(NT):
                    last = pe.matmul(ps_g[:, D * c:D * c + D], wET[:, P * c:P * c + P], lnb[:, :],
                                     start=True, stop=True)
                last.then_inc(s_wb, 1)

            def up(u):
                b, e = u.item, u.v
                if e == 0:
                    pe.wait_ge(s_xhi, b.count(1, 1))
                    pe.wait_ge(s_xlo, b.count(1, 1))
                if b.before(1):
                    pe.wait_ge(s_wh, 2 * e + 2)
                if not u.before(2):
                    pe.wait_ge(s_gelu, u.ago(2).count(1, 1))
                for m in range(MF):
                    for k in range(KD):
                        last = split3(pe, ps_h[u.par][:, m // 2, L * (m % 2):L * (m % 2) + L],
                                      (w1_hi[:, e, k, P * m:P * m + P], w1_lo[:, e, k, P * m:P * m + P]),
                                      (xT_hi[:, b.par, k, :], xT_lo[:, b.par, k, :]), k == 0, k == KD - 1)
                last.then_inc(s_h, 1)

            def down(u):
                b, e = u.item, u.v
                if b.before(1):
                    pe.wait_ge(s_wl, 2 * e + 2)
                pe.wait_ge(s_hlo, u.count(1, 1))
                if not u.before(2):
                    pe.wait_ge(s_y, u.ago(2).count(NT, NT))
                for c in range(NT):
                    for m in range(MF):
                        at = slice(L * m + P * c, L * m + P * c + P)
                        last = split3(pe, ps_o[u.par][:, D * c:D * c + D], (h_hi[:, u.par, at], h_lo[:, u.par, at]),
                                      (w2_hi[:, e, m, :], w2_lo[:, e, m, :]), m == 0, m == MF - 1)
                last.then_inc(s_o, 1)

            run_steps(pe, n_seq, by_unit([(up, 0, 1), (down, 1, 1)],
                                         {0: [(turn_x, 0)], 1: [(gate, 0)], 5: [(turn_w, 0)], 6: [(bias_w, 0)]}))

        @block.scalar
        def _(act):
            act.wait_ge(s_c, 16 * 6)

            def x_full(b):
                act.wait_ge(s_x, b.count(1, 1))
                if not b.before(1):
                    act.wait_ge(s_g, b.ago(1).count(1, 1))
                    act.wait_ge(s_xlo, b.ago(1).count(1, 1))
                    act.wait_ge(s_xhi, b.ago(1).count(1, 1))
                act.activation(xT_f[:, :, :].rearrange("p k t -> p (k t)"), ps_x[:, :], ACT.Copy).then_inc(s_xf, 1)

            def exp_gap(b):
                act.wait_ge(s_gap, b.count(1, 1))
                if not b.before(1):
                    act.wait_ge(s_w2, b.ago(1).count(1, 1))
                act.activation(e2[:, :], gap[:, :], ACT.Exp).then_inc(s_e2, 1)

            def copy_w(b):
                act.wait_ge(s_wt, b.count(1, 1))
                if not b.before(1):
                    act.wait_ge(s_wb, b.ago(1).count(1, 1))
                act.activation(wET[:, :], ps_g[0:E, 0:L], ACT.Copy).then_inc(s_wtc, 1)

            def gelu(u):
                act.wait_ge(s_h, u.count(1, 1))
                if not u.before(1):
                    act.wait_ge(s_hlo, u.ago(1).count(1, 1))
                    act.wait_ge(s_hhi, u.ago(1).count(1, 1))
                for m in range(MF):
                    last = act.activation(hid[:, L * m:L * m + L],
                                          ps_h[u.par][:, m // 2, L * (m % 2):L * (m % 2) + L], ACT.Gelu,
                                          bias=b1_c[:, u.v, m:m + 1])
                last.then_inc(s_gelu, 1)

            def h_high(u):
                act.wait_ge(s_gelu, u.count(1, 1))
                if not u.before(2):
                    act.wait_ge(s_o, u.ago(2).count(1, 1))
                act.activation(h_hi[:, u.par, :], hid[:, :], ACT.Copy).then_inc(s_hhi, 1)

            run_steps(act, n_seq, by_unit([(gelu, 0, 1), (h_high, 0, 1)],
                                          {0: [(x_full, 0)], 3: [(exp_gap, 0)], 5: [(copy_w, 0)]}))

        @block.vector
        def _(dve):
            dve.memset(pow_half[:, :], -0.5).then_inc(s_one, 1)
            dve.memset(ln_e_eps[:, :], LN_E).then_inc(s_one, 1)
            dve.memset(ln_eps[:, :], LN_EPS).then_inc(s_one, 1)
            for e in range(E):
                for j, (hi, lo, s_split) in enumerate(((w1_hi, w1_lo, s_wh), (w2_hi, w2_lo, s_wl))):
                    dve.wait_ge(s_w[j], 16 * e + 16)
                    src = stage[:, j, :]
                    hi_e = hi[:, e, :, :].rearrange("p k n -> p (k n)")
                    dve.tensor_copy(hi_e, src).then_inc(s_split, 1)
                    dve.wait_ge(s_split, 2 * e + 1)
                    dve.tensor_tensor(lo[:, e, :, :].rearrange("p k n -> p (k n)"), src, hi_e.bitcast(F32),
                                      ALU.subtract).then_inc(s_split, 1)
            dve.wait_ge(s_c, 16 * 6)
            dve.wait_ge(s_one, 4)

            def x_high(b):
                dve.wait_ge(s_xf, b.count(1, 1))
                if not b.before(2):
                    dve.wait_ge(s_h, b.ago(2).count(E, E))
                dve.tensor_copy(xT_hi[:, b.par, :, :], xT_f[:, :, :]).then_inc(s_xhi, 1)

            def route(b):
                dve.wait_ge(s_g, b.count(1, 1))
                if not b.before(1):
                    dve.wait_ge(s_idx, b.ago(1).count(NT, NT))
                    dve.wait_ge(s_gap, b.ago(1).count(1, 1))
                dve.tensor_copy(sg[:, :, :].rearrange("p c e -> p (c e)"), ps_g[:, 0:NT * E]).then_inc(s_sg, 1)
                wait_apart(dve, spare[0:1, :], (s_sg, b.count(1, 1)))
                for c in range(NT):
                    dve.max(top[:, c, :], sg[:, c, :]).then_inc(s_top, 1)
                free = [] if b.before(1) else [(s_if, b.ago(1).count(1, 1))]
                wait_apart(dve, spare[0:1, :], (s_top, b.count(NT, NT)), *free)
                for c in range(NT):
                    dve.max_index(idx[:, c, :], top[:, c, :], sg[:, c, :]).then_inc(s_idx, 1)
                if not b.before(1):
                    dve.wait_ge(s_e2, b.ago(1).count(1, 1))
                dve.tensor_tensor(gap[:, :], top[:, :, 1], top[:, :, 0], ALU.subtract).then_inc(s_gap, 1)
                dve.wait_ge(s_idx, b.count(NT, NT))
                if not b.before(1):
                    dve.wait_ge(s_pick, b.ago(1).count(2 * NT, 2 * NT))
                dve.tensor_copy(idx_f[:, :, :], idx[:, :, 0:2]).then_inc(s_if, 1)

            def weights(b):
                dve.wait_ge(s_e2, b.count(1, 1))
                dve.tensor_scalar(e2p[:, :], e2[:, :], 1.0, None, ALU.add).then_inc(s_p1, 1)
                dve.wait_ge(s_p1, b.count(1, 1))
                if not b.before(1):
                    dve.wait_ge(s_pick, b.ago(1).count(2 * NT, 2 * NT))
                dve.reciprocal(wt[:, :, 0], e2p[:, :]).then_inc(s_r, 1)
                dve.wait_ge(s_r, b.count(1, 1))
                dve.tensor_tensor(wt[:, :, 1], e2[:, :], wt[:, :, 0], ALU.mult).then_inc(s_w2, 1)
                dve.wait_ge(s_if, b.count(1, 1))
                dve.wait_ge(s_w2, b.count(1, 1))
                if not b.before(1):
                    dve.wait_ge(s_wE, b.ago(1).count(1, 1))
                for c in range(NT):
                    for n in range(2):
                        dve.tensor_scalar(pick[:, c, n, :], iota_e[:, :], idx_f[:, c, n:n + 1], wt[:, c, n:n + 1],
                                          ALU.is_equal, ALU.mult).then_inc(s_pick, 1)
                dve.wait_ge(s_pick, b.count(2 * NT, 2 * NT))
                if not b.before(2):
                    dve.wait_ge(s_sc, b.ago(2).count(E, E))
                    dve.wait_ge(s_wt, b.ago(2).count(1, 1))
                dve.tensor_tensor(wE[:, b.par, :, :], pick[:, :, 0, :], pick[:, :, 1, :], ALU.add).then_inc(s_wE, 1)

            def start_acc(b):
                dve.wait_ge(s_wb, b.count(1, 1))
                if not b.before(2):
                    dve.wait_ge(s_fo, b.ago(2).count(NT, NT))
                for c in range(NT):
                    dve.tensor_tensor(acc[:, b.par, c, :], ps_g[:, D * c:D * c + D], xa[:, b.par, c, :], ALU.add
                                      ).then_inc(s_a0, 1)

            def h_low(u):
                dve.wait_ge(s_hhi, u.count(1, 1))
                if not u.before(2):
                    dve.wait_ge(s_o, u.ago(2).count(1, 1))
                dve.tensor_tensor(h_lo[:, u.par, :], hid[:, :], h_hi[:, u.par, :].bitcast(F32), ALU.subtract
                                  ).then_inc(s_hlo, 1)

            def centre(u):
                dve.wait_ge(s_o, u.count(1, 1))
                dve.wait_ge(s_xb, u.count(1, 1))
                if not u.before(1):
                    dve.wait_ge(s_t, u.ago(1).count(NT, NT))
                for c in range(NT):
                    dve.tensor_tensor(yy[:, c, :], ps_o[u.par][:, D * c:D * c + D], xb[:, u.par, c, :], ALU.add
                                      ).then_inc(s_y, 1)
                for c in range(NT):
                    dve.wait_ge(s_y, u.count(NT, c + 1))
                    dve.bn_stats(st[:, c, :], yy[:, c, :]).then_inc(s_st, 1)
                free = [] if u.before(2) else [(s_ve, u.ago(2).count(1, 1))]
                wait_apart(dve, spare[0:1, :], (s_st, u.count(NT, NT)), *free)
                for c in range(NT):
                    dve.bn_aggr(mv[:, u.par, c, :], st[:, c, :]).then_inc(s_mv, 1)
                if not u.before(2):
                    dve.wait_ge(s_acc, u.ago(2).count(NT, NT))
                for c in range(NT):
                    dve.wait_ge(s_mv, u.count(NT, c + 1))
                    dve.scalar_tensor_tensor(out=tt[:, u.par, c, :], in0=yy[:, c, :], scalar=mv[:, u.par, c, 0:1],
                                             in1=g_b[:, u.v, :], op0=ALU.subtract, op1=ALU.mult).then_inc(s_t, 1)

            def add_up(u):
                b = u.item
                dve.wait_ge(s_sc, u.count(1, 1))
                if u.v == 0:
                    dve.wait_ge(s_a0, b.count(NT, NT))
                for c in range(NT):
                    if u.v:
                        dve.wait_ge(s_acc, u.ago(1).count(NT, c + 1))
                    dve.scalar_tensor_tensor(out=acc[:, b.par, c, :], in0=tt[:, u.par, c, :],
                                             scalar=sc[:, u.par, c:c + 1], in1=acc[:, b.par, c, :],
                                             op0=ALU.mult, op1=ALU.add).then_inc(s_acc, 1)

            def finish(b):
                dve.wait_ge(s_acc, b.count(E * NT, E * NT))
                for c in range(NT):
                    dve.bn_stats(fst[:, c, :], acc[:, b.par, c, :]).then_inc(s_fst, 1)
                free = [] if b.before(1) else [(s_fve, b.ago(1).count(1, 1))]
                wait_apart(dve, spare[0:1, :], (s_fst, b.count(NT, NT)), *free)
                for c in range(NT):
                    dve.bn_aggr(fmv[:, c, :], fst[:, c, :]).then_inc(s_fmv, 1)

            def normalise(b):
                dve.wait_ge(s_frs, b.count(1, 1))
                if not b.before(1):
                    dve.wait_ge(s_o_out, b.count(16, 0))
                for c in range(NT):
                    dve.tensor_scalar(o_t[:, c, :], acc[:, b.par, c, :], fmv[:, c, 0:1], frs[:, c:c + 1],
                                      ALU.subtract, ALU.mult).then_inc(s_fo, 1)

            run_steps(dve, n_seq, by_unit([(h_low, 0, 1), (centre, 1, 1), (add_up, 2, 1)],
                                          {1: [(x_high, 0), (finish, 2)], 2: [(route, 0), (normalise, 2)],
                                           4: [(weights, 0)], 6: [(start_acc, 0)]}))

        @block.gpsimd
        def _(pool):
            for e in range(E):
                last = pool.memset(iota_e[:, e:e + 1], float(e))
            last.then_inc(s_one, 1)
            pool.wait_ge(s_c, 16 * 6)
            pool.wait_ge(s_one, 4)

            def x_low(b):
                pool.wait_ge(s_xhi, b.count(1, 1))
                if not b.before(2):
                    pool.wait_ge(s_h, b.ago(2).count(E, E))
                pool.tensor_tensor(xT_lo[:, b.par, :, :], xT_f[:, :, :], xT_hi[:, b.par, :, :].bitcast(F32),
                                   ALU.subtract).then_inc(s_xlo, 1)

            def add_b2(u):
                b = u.item
                if u.v == 0:
                    pool.wait_ge(s_xa_in[b.par], b.half * 16 + 16)
                if not u.before(2):
                    pool.wait_ge(s_y, u.ago(2).count(NT, NT))
                pool.tensor_tensor(xb[:, u.par, :, :], xa[:, b.par, :, :],
                                   b2_b[:, u.v, :].unsqueeze(1).to_broadcast([P, NT, D]), ALU.add).then_inc(s_xb, 1)

            def scale(u):
                b = u.item
                pool.wait_ge(s_mv, u.count(NT, NT))
                pool.wait_ge(s_wE, b.count(1, 1))
                if not u.before(1):
                    pool.wait_ge(s_rs, u.ago(1).count(1, 1))
                pool.tensor_tensor(ve[:, :], mv[:, u.par, :, 1], ln_e_eps[:, :], ALU.add).then_inc(s_ve, 1)
                pool.wait_ge(s_ve, u.count(1, 1))
                if not u.before(1):
                    pool.wait_ge(s_sc, u.ago(1).count(1, 1))
                pool.tensor_tensor(rs[:, :], ve[:, :], pow_half[:, :], ALU.pow).then_inc(s_rs, 1)
                pool.wait_ge(s_rs, u.count(1, 1))
                if not u.before(2):
                    pool.wait_ge(s_acc, u.ago(2).count(NT, NT))
                pool.tensor_tensor(sc[:, u.par, :], rs[:, :], wE[:, b.par, :, u.v], ALU.mult).then_inc(s_sc, 1)

            def inv_std(b):
                pool.wait_ge(s_fmv, b.count(NT, NT))
                if not b.before(1):
                    pool.wait_ge(s_frs, b.ago(1).count(1, 1))
                pool.tensor_tensor(fve[:, :], fmv[:, :, 1], ln_eps[:, :], ALU.add).then_inc(s_fve, 1)
                pool.wait_ge(s_fve, b.count(1, 1))
                if not b.before(1):
                    pool.wait_ge(s_fo, b.ago(1).count(NT, NT))
                pool.tensor_tensor(frs[:, :], fve[:, :], pow_half[:, :], ALU.pow).then_inc(s_frs, 1)

            run_steps(pool, n_seq, by_unit([(add_b2, 0, 1), (scale, 1, 1)], {1: [(x_low, 0), (inv_std, 2)]}))


def program(nc, n_seq, xT, x, ctxT, a_w_in, a_w_out, a_norm_w, a_conv_w, a_conv_b, a_A_log, a_D_param, a_dt_bias,
            b_wq, b_bq, b_wk, b_bk, b_wv, b_bv, b_wo, b_bo, c_gate_w, c_w1, c_b1, c_w2, c_b2, c_ln_g, c_ln_b,
            masks, out):
    x1 = nc.dram_tensor("x1_scratch", [n_seq * L, D], F32).ap()
    x2 = nc.dram_tensor("x2_scratch", [n_seq * L, D], F32).ap()
    mixer_phase(nc, n_seq, xT, x, x1, a_w_in, a_w_out, a_norm_w, a_conv_w, a_conv_b, a_A_log, a_D_param, a_dt_bias,
                masks)
    attention_phase(nc, n_seq, x1, ctxT, x2, b_wq, b_bq, b_wk, b_bk, b_wv, b_bv, b_wo, b_bo, masks)
    experts_phase(nc, n_seq, x2, out, c_gate_w, c_w1, c_b1, c_w2, c_b2, c_ln_g, c_ln_b, masks)


def layouts(inputs):
    c = np.ascontiguousarray
    a = {k: np.asarray(v) for k, v in inputs.items()}

    def turned(m):
        return c(m.reshape(-1, KD, P).transpose(2, 1, 0))

    def columns(v):
        return c(np.moveaxis(v.reshape(*v.shape[:-1], -1, P), -1, 0))

    x = a["x"].reshape(-1, D)
    w = a["L0_attn_in_proj_w"].T
    di, h, n = 512, 8, 64
    z, xc, dt, b_, c_ = np.split(w, [di, 2 * di, 2 * di + h, 2 * di + h + n], axis=1)
    row, col = np.arange(P)[:, None], np.arange(P)[None, :]
    at, xat, ffn = ({k[len(p):]: v for k, v in a.items() if k.startswith(p)} for p in ("L0_attn_", "L0_xattn_", "L0_ffn_"))
    return {
        "xT": turned(x), "x": c(x), "ctxT": turned(a["ctx_1024"].reshape(-1, D)),
        "a_w_in": c(np.concatenate([z, xc, b_, c_, c_, b_, dt], axis=1)),
        "a_w_out": c(at["out_proj_w"].T), "a_norm_w": columns(at["norm_w"]),
        "a_conv_w": c(at["conv_w"].reshape(-1, P, 4).transpose(1, 0, 2)), "a_conv_b": columns(at["conv_b"]),
        "a_A_log": at["A_log"], "a_D_param": at["D_param"], "a_dt_bias": at["dt_bias"],
        "b_wq": c(xat["Wq"].T), "b_bq": columns(xat["bq"]), "b_wk": c(xat["Wk"].T), "b_bk": columns(xat["bk"]),
        "b_wv": c(xat["Wv"].T), "b_bv": xat["bv"], "b_wo": c(xat["Wo"].T), "b_bo": xat["bo"],
        "c_gate_w": ffn["gate_w"], "c_w1": ffn["w1"], "c_b1": columns(ffn["b1"]), "c_w2": ffn["w2"],
        "c_b2": ffn["b2"], "c_ln_g": ffn["ln_g"], "c_ln_b": ffn["ln_b"],
        "masks": np.stack([row <= col, row > col, row == col], axis=1).astype(np.float32),
    }


def kernel(**inputs):
    import concourse.bacc as bacc
    from concourse.bass_utils import run_bass_kernel_spmd

    nc = bacc.Bacc("TRN2", target_bir_lowering=False, num_devices=1)
    shape = inputs["x"].shape
    arrays = layouts(inputs)
    aps = {k: nc.dram_tensor(f"in_{k}", v.shape, mybir.dt.from_np(v.dtype), kind="ExternalInput").ap()
           for k, v in arrays.items()}
    out = nc.dram_tensor("out_0", (shape[0] * shape[1], shape[2]), F32, kind="ExternalOutput").ap()
    program(nc, shape[0], out=out, **aps)
    r = run_bass_kernel_spmd(nc, [{f"in_{k}": v for k, v in arrays.items()}], core_ids=[0])
    return r.results[0]["out_0"].reshape(shape)
```

```python
import math
from contextlib import ExitStack

import numpy as np

import concourse.bass as bass
from concourse import mybir

ALU = mybir.AluOpType
ACT = mybir.ActivationFunctionType
AX = mybir.AxisListType
F32 = mybir.dt.float32
F32R = mybir.dt.float32r
U32 = mybir.dt.uint32

P = 128
D = 256
L = 256
KD = D // P
NT = L // P
PEEL = 4


class Item:

    def __init__(self, half, par):
        self.half, self.par = half, par

    def ago(self, n):
        return Item(self.half + (self.par - n) // 2, (self.par - n) % 2)

    def known(self):
        return isinstance(self.half, int)

    def value(self):
        return 2 * self.half + self.par

    def before(self, n):
        return self.known() and self.value() < n

    def count(self, per, done):
        return self.half * (2 * per) + (self.par * per + done)


def run_steps(eng, n, stages, spare=0):
    last = max(lag for _, lag in stages)

    def peeled(s):
        for stage, lag in stages:
            if 0 <= s - lag < n:
                stage(Item(*divmod(s - lag, 2)))

    for s in range(PEEL):
        peeled(s)
    with eng.Fori(PEEL // 2, (n - spare) // 2) as pair:
        for par in (0, 1):
            for stage, lag in stages:
                stage(Item(pair, par).ago(lag))
    for s in range(n - spare, n + last):
        peeled(s)


def wait_apart(dve, spare, *waits):
    for semaphore, value in waits:
        dve.wait_ge(semaphore, value)
    dve.memset(spare, 0.0)


def split3(eng, out, lhs, rhs, start, stop):
    (lh, ll), (rh, rl) = lhs, rhs
    eng.matmul(out, lh, rh, start=start, stop=False)
    eng.matmul(out, lh, rl, start=False, stop=False)
    return eng.matmul(out, ll, rh, start=False, stop=stop)


def mixer_phase(nc, n_seq, following, xT, x, x1, w_in, w_out, norm_w, conv_w, conv_b, A_log, D_param, dt_bias, masks):
    H, N_STATE, D_CONV, DI = 8, 64, 4, 512
    HD = DI // H
    MI = DI // P
    C_Z, C_X, C_BC, C_DT = 0, DI, 2 * DI, 2 * DI + 4 * N_STATE
    W_IN = C_DT + H
    RMS_EPS, LN_EPS = 1e-6, 1e-5

    with ExitStack() as ctx:
        def sb(name, shape, dt=F32):
            return ctx.enter_context(nc.sbuf_tensor("a_" + name, shape, dt))

        def sem(name):
            return ctx.enter_context(nc.semaphore("a_" + name))

        w_stage = sb("w_stage", [P, KD, W_IN])
        w_hi = sb("w_hi", [P, KD, C_DT], F32R)
        w_lo = sb("w_lo", [P, KD, C_DT], F32R)
        wo_stage = sb("wo_stage", [P, MI, D])
        wo_hi = sb("wo_hi", [P, MI, D], F32R)
        wo_lo = sb("wo_lo", [P, MI, D], F32R)
        nw = sb("nw", [P, MI])
        cw = sb("cw", [P, MI, D_CONV])
        cb = sb("cb", [P, MI])
        a_neg = sb("a_neg", [P, H])
        d_b = sb("d_b", [P, H])
        dtb = sb("dtb", [P, H])
        mk = sb("mk", [P, 3, P])
        upto, after, ident = mk[:, 0, :], mk[:, 1, :], mk[:, 2, :]
        spare = sb("spare", [P, 1])
        pow_half = sb("pow_half", [P, NT])
        rms_eps = sb("rms_eps", [P, NT])
        ln_eps = sb("ln_eps", [P, NT])

        xT_f = sb("xT_f", [P, 2, KD, L])
        xT_hi = sb("xT_hi", [P, 2, KD, L], F32R)
        xT_lo = sb("xT_lo", [P, 2, KD, L], F32R)
        x_f = sb("x_f", [P, 2, NT, D])
        xc_pad = sb("xc_pad", [P, MI, L + D_CONV - 1])
        conv = sb("conv", [P, MI, L])
        conv_t = sb("conv_t", [P, MI, L])
        sx = sb("sx", [P, 2, MI, L])
        z_t = sb("z_t", [P, NT, DI])
        zs = sb("zs", [P, 2, NT, DI])
        bc = sb("bc", [N_STATE, 2, 2, L])
        v_dt = sb("v_dt", [P, NT * H])
        v_na = sb("v_na", [P, NT * H])
        v_ex = sb("v_ex", [P, NT * H])
        v_ln = sb("v_ln", [P, NT * H])
        v_sp = sb("v_sp", [P, NT * H])
        l_dt = sb("l_dt", [P, 2, NT * H])
        lm = sb("lm", [P, NT, H, P])
        g_m = sb("g_m", [P, 3, P])
        e_x = sb("e_x", [P, NT, H, P])
        mt = sb("mt", [P, NT, H, P])
        x_t = sb("x_t", [P, NT, DI])
        xd = sb("xd", [P, NT, DI])
        cx = sb("cx", [P, DI])
        rc = sb("rc", [P, 2 * H])
        t1 = sb("t1", [P, NT, DI])
        off_r = sb("off_r", [P, DI])
        t2 = sb("t2", [P, DI])
        y = sb("y", [P, 2, NT, DI])
        sq = sb("sq", [P, DI])
        ss = sb("ss", [P, 2, NT])
        ms = sb("ms", [P, NT])
        rinv = sb("rinv", [P, 2, NT])
        yT_hi = sb("yT_hi", [P, MI, L], F32R)
        yT_lo = sb("yT_lo", [P, MI, L], F32R)
        res = sb("res", [P, NT, D])
        st = sb("st", [P, NT, 6])
        mv = sb("mv", [P, NT, 2])
        ve = sb("ve", [P, NT])
        rstd = sb("rstd", [P, NT])
        x1_t = sb("x1_t", [P, 2, NT, D])

        p01 = ctx.enter_context(nc.psum_tensor("a_p01", [P, 2, 512], F32))
        p23 = ctx.enter_context(nc.psum_tensor("a_p23", [P, 2, 512], F32))
        p45 = ctx.enter_context(nc.psum_tensor("a_p45", [P, 2, 512], F32))
        p6 = ctx.enter_context(nc.psum_tensor("a_p6", [P, 512], F32))
        p7 = ctx.enter_context(nc.psum_tensor("a_p7", [P, 512], F32))
        ps_xc = p01[:, :, :].rearrange("p b (m t) -> p (b m) t", m=2)
        ps_yT = p23[:, :, :].rearrange("p b (m t) -> p (b m) t", m=2)
        ps_bc = p6[:, :].rearrange("p (w t) -> p w t", w=2)
        ps_out = p6[:, :].rearrange("p (c d) -> p c d", c=NT)
        ps_g = p7[:, 0:3 * P].rearrange("p (g t) -> p g t", g=3)
        ps_dt = p7[:, 3 * P:3 * P + NT * H]
        ps_rc = p7[:, 3 * P + NT * H:3 * P + NT * H + 2 * H]

        s_load = sem("load")
        s_w_in = sem("w_in")
        s_wprep = sem("wprep")
        s_wout = sem("wout")
        s_whi_a = sem("whi_a")
        s_pow = sem("pow")
        s_xT_in = [sem("xT_in0"), sem("xT_in1")]
        s_x_in = [sem("x_in0"), sem("x_in1")]
        s_x1_out = [sem("x1_out0"), sem("x1_out1")]
        s_xc, s_z, s_yT, s_bc, s_small, s_g, s_E, s_T, s_out, s_Y, s_off = (
            sem(n) for n in ("xc", "z", "yT", "bc", "small", "g", "E", "T", "out", "Y", "off"))
        s_pad, s_tap, s_sq, s_yhi, s_zt, s_bcc, s_rc, s_exp, s_xt, s_ct, s_dex, s_dln = (
            sem(n) for n in ("pad", "tap", "sq", "yhi", "zt", "bcc", "rc", "exp", "xt", "ct", "dex", "dln"))
        s_xhi, s_conv, s_ylo, s_zs, s_v, s_na, s_gm, s_mt, s_sx, s_sp, s_l, s_res, s_st, s_mv, s_x1, s_t1, s_or = (
            sem(n) for n in ("xhi", "conv", "ylo", "zs", "v", "na", "gm", "mt", "sx", "sp", "l", "res", "st",
                             "mv", "x1", "t1", "or"))
        s_xlo, s_cx, s_xd, s_lm, s_t2, s_y, s_ri, s_ve, s_rs = (
            sem(n) for n in ("xlo", "cx", "xd", "lm", "t2", "y", "ri", "ve", "rs"))

        N_LOADS = 8
        W_PARTS = (slice(C_X, C_X + DI), slice(C_BC, C_DT), slice(C_Z, C_Z + DI))

        block = ctx.enter_context(nc.Block())

        @block.sync
        def _(sp):
            sp.dma_start(w_stage[:, :, :], w_in.rearrange("(k p) n -> p k n", p=P)).then_inc(s_w_in, 16)
            sp.dma_start(xT_f[:, 0, :, :], xT[:, :, 0:L]).then_inc(s_xT_in[0], 16)
            sp.dma_start(wo_stage[:, :, :], w_out.rearrange("(k p) n -> p k n", p=P)).then_inc(s_load, 16)
            sp.dma_start(nw[:, :], norm_w).then_inc(s_load, 16)
            sp.dma_start(cw[:, :, :], conv_w).then_inc(s_load, 16)
            sp.dma_start(cb[:, :], conv_b).then_inc(s_load, 16)
            sp.dma_start(a_neg[:, :], A_log.partition_broadcast(P)).then_inc(s_load, 16)
            sp.dma_start(d_b[:, :], D_param.partition_broadcast(P)).then_inc(s_load, 16)
            sp.dma_start(dtb[:, :], dt_bias.partition_broadcast(P)).then_inc(s_load, 16)
            sp.dma_start(mk[:, :, :], masks).then_inc(s_load, 16)

            def load_xT(b):
                if not b.before(2):
                    sp.wait_ge(s_xhi, b.ago(2).count(1, 1))
                    sp.wait_ge(s_xlo, b.ago(2).count(1, 1))
                    sp.wait_ge(s_small, b.ago(2).count(1, 1))
                sp.dma_start(xT_f[:, b.par, :, :], xT[:, :, bass.ds(b.value() * L, L)]).then_inc(s_xT_in[b.par], 16)

            def load_x(b):
                if not b.before(2):
                    sp.wait_ge(s_res, b.ago(2).count(NT, NT))
                sp.dma_start(x_f[:, b.par, :, :], x[bass.ds(b.value() * L, L), :].rearrange("(c p) d -> p c d", p=P)
                             ).then_inc(s_x_in[b.par], 16)

            def store(b):
                sp.wait_ge(s_x1, b.count(NT, NT))
                sp.dma_start(x1[bass.ds(b.value() * L, L), :].rearrange("(c p) d -> p c d", p=P), x1_t[:, b.par, :, :]
                             ).then_inc(s_x1_out[b.par], 16)

            def load_xT_ahead(b):
                if b.value() + 2 < n_seq if b.known() else True:
                    load_xT(b.ago(-2))

            load_xT(Item(0, 1))
            following.load(sp)
            run_steps(sp, n_seq, [(store, 3), (load_xT_ahead, 0), (load_x, 0)], spare=2)
            for par in (0, 1):
                sp.wait_ge(s_x1_out[par], 16 * (n_seq // 2))

        @block.tensor
        def _(pe):
            def pair(hi, lo, *at):
                return hi[at], lo[at]

            def in_x(b):
                if b.before(1):
                    pe.wait_ge(s_wprep, 1)
                pe.wait_ge(s_xhi, b.count(1, 1))
                pe.wait_ge(s_xlo, b.count(1, 1))
                if b.known() and b.value() == 1:
                    pe.wait_ge(s_tap, 1)
                for m in range(MI):
                    if not b.before(2) and m % 2 == 0:
                        pe.wait_ge(s_t1, b.ago(2).count(NT, m // 2 + 1))
                    for k in range(KD):
                        last = split3(pe, ps_xc[:, m, :],
                                      pair(w_hi, w_lo, slice(None), k, slice(C_X + P * m, C_X + P * m + P)),
                                      pair(xT_hi, xT_lo, slice(None), b.par, k), k == 0, k == KD - 1)
                last.then_inc(s_xc, 1)

            def in_z(b):
                if b.before(1):
                    pe.wait_ge(s_wprep, 3)
                if not b.before(2):
                    pe.wait_ge(s_xt, b.ago(2).count(1, 1))
                elif b.value() == 1:
                    pe.wait_ge(s_zs, 1)
                for c in range(NT):
                    for k in range(KD):
                        last = split3(pe, p45[:, c, :],
                                      pair(xT_hi, xT_lo, slice(None), b.par, k, slice(P * c, P * c + P)),
                                      pair(w_hi, w_lo, slice(None), k, slice(C_Z, C_Z + DI)), k == 0, k == KD - 1)
                last.then_inc(s_z, 1)

            def in_bc(b):
                if b.before(1):
                    pe.wait_ge(s_wprep, 2)
                if not b.before(3):
                    pe.wait_ge(s_res, b.ago(3).count(NT, NT))
                elif not b.before(1):
                    pe.wait_ge(s_bcc, b.ago(1).count(1, 1))
                for w in range(2):
                    for k in range(KD):
                        last = split3(pe, ps_bc[:, w, :],
                                      pair(w_hi, w_lo, slice(None), k, slice(C_BC + P * w, C_BC + P * w + P)),
                                      pair(xT_hi, xT_lo, slice(None), b.par, k), k == 0, k == KD - 1)
                last.then_inc(s_bc, 1)

            def step_size(b):
                if not b.before(2):
                    pe.wait_ge(s_or, b.ago(2).count(1, 1))
                elif b.value() == 1:
                    pe.wait_ge(s_v, 1)
                for c in range(NT):
                    for k in range(KD):
                        last = pe.matmul(ps_dt[:, H * c:H * c + H], xT_f[:, b.par, k, P * c:P * c + P],
                                         w_stage[:, k, C_DT:W_IN], start=(k == 0), stop=(k == KD - 1))
                last.then_inc(s_small, 1)

            def scores(b):
                if b.before(1):
                    pe.wait_ge(s_load, 16 * N_LOADS)
                if b.known() and b.value() == n_seq - 1:
                    pe.wait_ge(s_or, b.ago(1).count(1, 1))
                pe.wait_ge(s_bcc, b.count(1, 1))
                pe.wait_ge(s_l, b.count(1, 1))
                bT, cT = bc[:, b.par, 0, :], bc[:, b.par, 1, :]
                pe.matmul(ps_g[:, 0:2, :].rearrange("p g t -> p (g t)"), bT[:, 0:P], cT, start=True, stop=True)
                pe.matmul(ps_g[:, 2, :], bT[:, P:L], cT[:, P:L], start=True, stop=True)
                pe.matmul(ps_rc[:, 0:H], upto, l_dt[:, b.par, H:2 * H], start=True, stop=True)
                pe.matmul(ps_rc[:, H:2 * H], after, l_dt[:, b.par, 0:H], start=True, stop=True).then_inc(s_g, 1)

            def decay(c):
                def run(b):
                    if c == 0:
                        pe.wait_ge(s_lm, b.count(1, 1))
                        if not b.before(1):
                            pe.wait_ge(s_ylo, b.ago(1).count(1, 1))
                    else:
                        pe.wait_ge(s_exp, b.count(NT, 1))
                    for j in range(2):
                        last = pe.matmul(p23[:, j, :], after,
                                         lm[:, c, 4 * j:4 * j + 4, :].rearrange("p h t -> p (h t)"),
                                         start=True, stop=True)
                    last.then_inc(s_E, 1)
                return run

            def turn_x(b):
                pe.wait_ge(s_sx, b.count(1, 1))
                if b.known() and b.value() == n_seq - 1:
                    pe.wait_ge(s_xt, b.ago(1).count(1, 1))
                else:
                    pe.wait_ge(s_zs, b.ago(-1).count(1, 1))
                for c in range(NT):
                    for m in range(MI):
                        last = pe.transpose(p45[:, c, P * m:P * m + P], sx[:, b.par, m, P * c:P * c + P], ident)
                last.then_inc(s_T, 1)

            def mix(b):
                if b.known() and b.value() == n_seq - 1:
                    pe.wait_ge(s_t1, b.ago(1).count(NT, NT))
                else:
                    pe.wait_ge(s_tap, b.ago(-1).count(1, 1))
                pe.wait_ge(s_xt, b.count(1, 1))
                for c in range(NT):
                    pe.wait_ge(s_mt, b.count(NT, c + 1))
                    for h in range(H):
                        last = pe.matmul(p01[:, c, HD * h:HD * h + HD], mt[:, c, h, :], x_t[:, c, HD * h:HD * h + HD],
                                         start=True, stop=True)
                    last.then_inc(s_Y, 1)

            def mix_off(b):
                pe.wait_ge(s_cx, b.count(1, 1))
                pe.wait_ge(s_rc, b.count(1, 1))
                pe.matmul(p7[:, :], g_m[:, 1, :], cx[:, :], start=True, stop=True).then_inc(s_off, 1)

            def turn_y(b):
                pe.wait_ge(s_y, b.count(NT, NT))
                pe.wait_ge(s_exp, b.count(NT, NT))
                for m in range(MI):
                    for c in range(NT):
                        last = pe.transpose(ps_yT[:, m, P * c:P * c + P], y[:, b.par, c, P * m:P * m + P], ident)
                last.then_inc(s_yT, 1)

            def out(b):
                if b.before(1):
                    pe.wait_ge(s_wout, MI + 2)
                pe.wait_ge(s_ylo, b.count(1, 1))
                if b.known() and b.value() >= n_seq - 2:
                    pe.wait_ge(s_res, b.ago(1).count(NT, NT))
                else:
                    pe.wait_ge(s_bcc, b.ago(-2).count(1, 1))
                for c in range(NT):
                    for m in range(MI):
                        last = split3(pe, ps_out[:, c, :], pair(yT_hi, yT_lo, slice(None), m, slice(P * c, P * c + P)),
                                      pair(wo_hi, wo_lo, slice(None), m), m == 0, m == MI - 1)
                last.then_inc(s_out, 1)

            run_steps(pe, n_seq, [
                (in_x, 0), (in_bc, 0), (turn_y, 2), (in_z, 0), (step_size, 0), (scores, 1), (decay(0), 1), (turn_x, 1),
                (decay(1), 1), (out, 2), (mix, 1), (mix_off, 1)])

        @block.scalar
        def _(act):
            act.wait_ge(s_w_in, 16)
            for part in W_PARTS:
                act.activation(w_hi[:, :, part], w_stage[:, :, part], ACT.Copy).then_inc(s_whi_a, 1)
            act.wait_ge(s_load, 16 * N_LOADS)
            act.activation(a_neg[:, :], a_neg[:, :], ACT.Exp).then_inc(s_whi_a, 1)

            def take_xc(b):
                act.wait_ge(s_xc, b.count(1, 1))
                if b.before(1):
                    act.wait_ge(s_pow, 2)
                else:
                    act.wait_ge(s_conv, b.ago(1).count(12, 12))
                    act.wait_ge(s_sx, b.ago(1).count(1, 1))
                act.activation(xc_pad[:, :, D_CONV - 1:], ps_xc, ACT.Copy).then_inc(s_pad, 1)
                for m in range(MI):
                    last = act.activation(conv[:, m, :], ps_xc[:, m, :], ACT.Identity,
                                          bias=cb[:, m:m + 1], scale=cw[:, m, D_CONV - 1:D_CONV])
                last.then_inc(s_tap, 1)

            def squares(b):
                for c in range(NT):
                    act.wait_ge(s_y, b.count(NT, c + 1))
                    if c:
                        act.wait_ge(s_sq, b.count(NT, c))
                    elif not b.before(1):
                        act.wait_ge(s_sq, b.ago(1).count(NT, NT))
                    if not b.before(2) and c == 0:
                        act.wait_ge(s_ri, b.ago(2).count(2, 1))
                    act.activation(sq[:, :], y[:, b.par, c, :], ACT.Square, accum_out=ss[:, b.par, c:c + 1]
                                   ).then_inc(s_sq, 1)

            def tanh_z(b):
                act.wait_ge(s_z, b.count(1, 1))
                if not b.before(1):
                    act.wait_ge(s_zs, b.ago(1).count(1, 1))
                act.activation(z_t[:, :, :], p45[:, :, :], ACT.Tanh, scale=0.5).then_inc(s_zt, 1)

            def y_high(b):
                act.wait_ge(s_yT, b.count(1, 1))
                if not b.before(1):
                    act.wait_ge(s_out, b.ago(1).count(1, 1))
                act.activation(yT_hi[:, :, :], ps_yT, ACT.Copy).then_inc(s_yhi, 1)

            def take_bc(b):
                act.wait_ge(s_bc, b.count(1, 1))
                if not b.before(2):
                    act.wait_ge(s_g, b.ago(2).count(1, 1))
                act.activation(bc[:, b.par, :, :], ps_bc[0:N_STATE, :, :], ACT.Copy).then_inc(s_bcc, 1)

            def exp_rc(b):
                act.wait_ge(s_g, b.count(1, 1))
                act.wait_ge(s_gm, b.count(1, 1))
                if not b.before(1):
                    act.wait_ge(s_or, b.ago(1).count(1, 1))
                    act.wait_ge(s_cx, b.ago(1).count(1, 1))
                act.activation(rc[:, :], ps_rc, ACT.Exp).then_inc(s_rc, 1)

            def exp_decay(c):
                def run(b):
                    act.wait_ge(s_E, b.count(NT, c + 1))
                    if not b.before(1):
                        act.wait_ge(s_mt, b.ago(1).count(NT, c + 1))
                    act.activation(e_x[:, c, :, :].rearrange("p h t -> p (h t)"),
                                   p23[:, :, :].rearrange("p b t -> p (b t)"), ACT.Exp).then_inc(s_exp, 1)
                return run

            def take_x(b):
                act.wait_ge(s_T, b.count(1, 1))
                if not b.before(1):
                    act.wait_ge(s_Y, b.ago(1).count(NT, NT))
                    act.wait_ge(s_xd, b.ago(1).count(1, 1))
                    act.wait_ge(s_cx, b.ago(1).count(1, 1))
                act.activation(x_t[:, :, :], p45[:, :, :], ACT.Copy).then_inc(s_xt, 1)

            def tanh_conv(b):
                act.wait_ge(s_conv, b.count(12, 12))
                if not b.before(1):
                    act.wait_ge(s_sx, b.ago(1).count(1, 1))
                act.activation(conv_t[:, :, :], conv[:, :, :], ACT.Tanh, scale=0.5).then_inc(s_ct, 1)

            def softplus(b):
                act.wait_ge(s_na, b.count(1, 1))
                act.activation(v_ex[:, :], v_na[:, :], ACT.Exp).then_inc(s_dex, 1)
                act.wait_ge(s_dex, b.count(1, 1))
                if not b.before(1):
                    act.wait_ge(s_sp, b.ago(1).count(1, 1))
                act.activation(v_ln[:, :], v_ex[:, :], ACT.Ln, bias=1.0).then_inc(s_dln, 1)

            run_steps(act, n_seq, [
                (take_xc, 0), (squares, 2), (y_high, 2), (tanh_z, 0), (take_bc, 0), (exp_decay(0), 1), (exp_rc, 1),
                (take_x, 1), (exp_decay(1), 1), (tanh_conv, 0), (softplus, 0)])

        @block.vector
        def _(dve):
            dve.memset(xc_pad[:, :, :], 0.0).then_inc(s_pow, 1)
            dve.memset(pow_half[:, :], -0.5).then_inc(s_pow, 1)
            dve.memset(rms_eps[:, :], 16 * DI * RMS_EPS).then_inc(s_pow, 1)
            dve.memset(ln_eps[:, :], LN_EPS).then_inc(s_pow, 1)

            def prep_out():
                for m in range(MI):
                    dve.tensor_scalar(wo_stage[:, m, :], wo_stage[:, m, :], nw[:, m:m + 1], DI ** 0.5,
                                      ALU.mult, ALU.mult).then_inc(s_wout, 1)
                dve.wait_ge(s_wout, MI)
                dve.tensor_copy(wo_hi[:, :, :], wo_stage[:, :, :]).then_inc(s_wout, 1)
                dve.wait_ge(s_wout, MI + 1)
                dve.tensor_tensor(wo_lo[:, :, :], wo_stage[:, :, :], wo_hi[:, :, :].bitcast(F32), ALU.subtract
                                  ).then_inc(s_wout, 1)

            def x_high(b):
                dve.wait_ge(s_xT_in[b.par], b.half * 16 + 16)
                if not b.before(2):
                    dve.wait_ge(s_bc, b.ago(2).count(1, 1))
                dve.tensor_copy(xT_hi[:, b.par, :, :], xT_f[:, b.par, :, :]).then_inc(s_xhi, 1)

            def taps(first, end):
                def run(b):
                    if first == 0:
                        dve.wait_ge(s_tap, b.count(1, 1))
                    for k in range(first, end):
                        for m in range(MI):
                            if k:
                                dve.wait_ge(s_conv, b.count(12, 4 * (k - 1) + m + 1))
                            dve.scalar_tensor_tensor(out=conv[:, m, :], in0=xc_pad[:, m, k:k + L],
                                                     scalar=cw[:, m, k:k + 1], in1=conv[:, m, :],
                                                     op0=ALU.mult, op1=ALU.add).then_inc(s_conv, 1)
                return run

            def gate(b):
                dve.wait_ge(s_zt, b.count(1, 1))
                if not b.before(2):
                    dve.wait_ge(s_y, b.ago(2).count(NT, NT))
                dve.scalar_tensor_tensor(out=zs[:, b.par, :, :], in0=z_t[:, :, :], scalar=1.0, in1=p45[:, :, :],
                                         op0=ALU.add, op1=ALU.mult).then_inc(s_zs, 1)

            def y_low(b):
                dve.wait_ge(s_yhi, b.count(1, 1))
                dve.tensor_tensor(yT_lo[:, :, :], ps_yT, yT_hi[:, :, :].bitcast(F32), ALU.subtract).then_inc(s_ylo, 1)

            def bias_dt(b):
                dve.wait_ge(s_small, b.count(1, 1))
                if not b.before(1):
                    dve.wait_ge(s_g, b.ago(1).count(1, 1))
                    dve.wait_ge(s_sp, b.ago(1).count(1, 1))
                dve.tensor_tensor(v_dt[:, :].rearrange("p (c h) -> p c h", c=NT),
                                  ps_dt.rearrange("p (c h) -> p c h", c=NT),
                                  dtb[:, :].unsqueeze(1).to_broadcast([P, NT, H]), ALU.add).then_inc(s_v, 1)
                dve.wait_ge(s_v, b.count(1, 1))
                if not b.before(1):
                    dve.wait_ge(s_dex, b.ago(1).count(1, 1))
                dve.scalar_tensor_tensor(out=v_na[:, :], in0=v_dt[:, :], scalar=-1.0, in1=v_dt[:, :],
                                         op0=ALU.mult, op1=ALU.min).then_inc(s_na, 1)

            def mask_g(b):
                dve.wait_ge(s_g, b.count(1, 1))
                if not b.before(1):
                    dve.wait_ge(s_off, b.ago(1).count(1, 1))
                dve.tensor_copy(g_m[:, 1, :], ps_g[:, 1, :])
                dve.tensor_tensor(g_m[:, 0:3:2, :], ps_g[:, 0:3:2, :], upto.unsqueeze(1).to_broadcast([P, 2, P]),
                                  ALU.mult).then_inc(s_gm, 1)

            def weigh(c):
                def run(b):
                    dve.wait_ge(s_exp, b.count(NT, c + 1))
                    dve.wait_ge(s_gm, b.count(1, 1))
                    if not b.before(1):
                        dve.wait_ge(s_Y, b.ago(1).count(NT, c + 1))
                    dve.tensor_tensor(mt[:, c, :, :], e_x[:, c, :, :],
                                      g_m[:, 2 * c, :].unsqueeze(1).to_broadcast([P, H, P]), ALU.mult
                                      ).then_inc(s_mt, 1)
                return run

            def silu_conv(b):
                dve.wait_ge(s_ct, b.count(1, 1))
                if not b.before(2):
                    dve.wait_ge(s_T, b.ago(2).count(1, 1))
                dve.scalar_tensor_tensor(out=sx[:, b.par, :, :], in0=conv_t[:, :, :], scalar=1.0, in1=conv[:, :, :],
                                         op0=ALU.add, op1=ALU.mult).then_inc(s_sx, 1)

            def log_decay(b):
                dve.wait_ge(s_dln, b.count(1, 1))
                dve.scalar_tensor_tensor(out=v_sp[:, :], in0=v_dt[:, :], scalar=0.0, in1=v_ln[:, :],
                                         op0=ALU.max, op1=ALU.add).then_inc(s_sp, 1)
                dve.wait_ge(s_sp, b.count(1, 1))
                if not b.before(2):
                    dve.wait_ge(s_lm, b.ago(2).count(1, 1))
                    dve.wait_ge(s_g, b.ago(2).count(1, 1))
                dve.tensor_tensor(l_dt[:, b.par, :].rearrange("p (c h) -> p c h", c=NT),
                                  v_sp[:, :].rearrange("p (c h) -> p c h", c=NT),
                                  a_neg[:, :].unsqueeze(1).to_broadcast([P, NT, H]), ALU.mult).then_inc(s_l, 1)

            def residual(b):
                dve.wait_ge(s_out, b.count(1, 1))
                dve.wait_ge(s_ri, b.count(2, 2))
                dve.wait_ge(s_x_in[b.par], b.half * 16 + 16)
                if not b.before(1):
                    dve.wait_ge(s_x1, b.ago(1).count(NT, NT))
                for c in range(NT):
                    dve.scalar_tensor_tensor(out=res[:, c, :], in0=ps_out[:, c, :], scalar=rinv[:, b.par, c:c + 1],
                                             in1=x_f[:, b.par, c, :], op0=ALU.mult, op1=ALU.add).then_inc(s_res, 1)
                for c in range(NT):
                    dve.wait_ge(s_res, b.count(NT, c + 1))
                    dve.bn_stats(st[:, c, :], res[:, c, :]).then_inc(s_st, 1)
                free = [] if b.before(1) else [(s_ve, b.ago(1).count(1, 1))]
                wait_apart(dve, spare[0:1, :], (s_st, b.count(NT, NT)), *free)
                for c in range(NT):
                    dve.bn_aggr(mv[:, c, :], st[:, c, :]).then_inc(s_mv, 1)

            def normalise(b):
                dve.wait_ge(s_rs, b.count(1, 1))
                if not b.before(2):
                    dve.wait_ge(s_x1_out[b.par], b.half * 16)
                for c in range(NT):
                    dve.tensor_scalar(x1_t[:, b.par, c, :], res[:, c, :], mv[:, c, 0:1], rstd[:, c:c + 1],
                                      ALU.subtract, ALU.mult).then_inc(s_x1, 1)

            def add_d(b):
                dve.wait_ge(s_xd, b.count(1, 1))
                for c in range(NT):
                    dve.wait_ge(s_Y, b.count(NT, c + 1))
                    if not b.before(1):
                        dve.wait_ge(s_y, b.ago(1).count(NT, NT))
                    dve.tensor_tensor(t1[:, c, :], p01[:, c, :], xd[:, c, :], ALU.add).then_inc(s_t1, 1)
                dve.wait_ge(s_off, b.count(1, 1))
                dve.wait_ge(s_rc, b.count(1, 1))
                if not b.before(1):
                    dve.wait_ge(s_t2, b.ago(1).count(1, 1))
                dve.tensor_tensor(off_r[:, :].rearrange("p (h d) -> p h d", h=H),
                                  p7[:, :].rearrange("p (h d) -> p h d", h=H),
                                  rc[:, 0:H].unsqueeze(2).to_broadcast([P, H, HD]), ALU.mult).then_inc(s_or, 1)

            x_high(Item(0, 0))
            for i, part in enumerate(W_PARTS):
                dve.wait_ge(s_whi_a, i + 1)
                dve.tensor_tensor(w_lo[:, :, part], w_stage[:, :, part], w_hi[:, :, part].bitcast(F32), ALU.subtract
                                  ).then_inc(s_wprep, 1)

            def x_high_next(b):
                if not (b.known() and b.value() + 1 >= n_seq):
                    x_high(b.ago(-1))

            def prep_once(b):
                if b.before(1):
                    dve.wait_ge(s_load, 16 * N_LOADS)
                    dve.wait_ge(s_whi_a, len(W_PARTS) + 1)
                    dve.tensor_scalar(a_neg[:, :], a_neg[:, :], -1.0, None, ALU.mult).then_inc(s_wprep, 1)
                    prep_out()

            run_steps(dve, n_seq, [
                (prep_once, 0), (x_high_next, 0), (taps(0, 1), 0), (y_low, 2), (gate, 0), (bias_dt, 0), (mask_g, 1),
                (taps(1, 3), 0), (weigh(0), 1), (weigh(1), 1), (silu_conv, 0), (log_decay, 0), (normalise, 3),
                (add_d, 1), (residual, 2)], spare=2)

        @block.gpsimd
        def _(pool):
            def x_low(b):
                pool.wait_ge(s_xhi, b.count(1, 1))
                if not b.before(2):
                    pool.wait_ge(s_bc, b.ago(2).count(1, 1))
                pool.tensor_tensor(xT_lo[:, b.par, :, :], xT_f[:, b.par, :, :], xT_hi[:, b.par, :, :].bitcast(F32),
                                   ALU.subtract).then_inc(s_xlo, 1)

            def scale_x(b):
                pool.wait_ge(s_xt, b.count(1, 1))
                pool.wait_ge(s_rc, b.count(1, 1))
                if not b.before(1):
                    pool.wait_ge(s_off, b.ago(1).count(1, 1))
                pool.tensor_tensor(cx[:, :].rearrange("p (h d) -> p h d", h=H),
                                   x_t[:, 0, :].rearrange("p (h d) -> p h d", h=H),
                                   rc[:, H:2 * H].unsqueeze(2).to_broadcast([P, H, HD]), ALU.mult).then_inc(s_cx, 1)
                if not b.before(1):
                    pool.wait_ge(s_t1, b.ago(1).count(NT, NT))
                for c in range(NT):
                    last = pool.tensor_tensor(xd[:, c, :].rearrange("p (h d) -> p h d", h=H),
                                              x_t[:, c, :].rearrange("p (h d) -> p h d", h=H),
                                              d_b[:, :].unsqueeze(2).to_broadcast([P, H, HD]), ALU.mult)
                last.then_inc(s_xd, 1)

            def spread_l(b):
                pool.wait_ge(s_l, b.count(1, 1))
                if not b.before(1):
                    pool.wait_ge(s_E, b.ago(1).count(NT, NT))
                for c in range(NT):
                    last = pool.tensor_tensor(lm[:, c, :, :],
                                              l_dt[:, b.par, H * c:H * c + H].unsqueeze(2).to_broadcast([P, H, P]),
                                              upto.unsqueeze(1).to_broadcast([P, H, P]), ALU.mult)
                last.then_inc(s_lm, 1)

            def join(b):
                pool.wait_ge(s_t1, b.count(NT, 1))
                if not b.before(2):
                    pool.wait_ge(s_yT, b.ago(2).count(1, 1))
                    pool.wait_ge(s_sq, b.ago(2).count(NT, NT))
                pool.wait_ge(s_zs, b.count(1, 1))
                pool.tensor_tensor(y[:, b.par, 0, :], t1[:, 0, :], zs[:, b.par, 0, :], ALU.mult).then_inc(s_y, 1)
                pool.wait_ge(s_or, b.count(1, 1))
                if not b.before(1):
                    pool.wait_ge(s_y, b.ago(1).count(NT, NT))
                pool.tensor_tensor(t2[:, :], t1[:, 1, :], off_r[:, :], ALU.add).then_inc(s_t2, 1)
                pool.wait_ge(s_t2, b.count(1, 1))
                pool.tensor_tensor(y[:, b.par, 1, :], t2[:, :], zs[:, b.par, 1, :], ALU.mult).then_inc(s_y, 1)

            def inv_rms(b):
                pool.wait_ge(s_sq, b.count(NT, NT))
                if not b.before(1):
                    pool.wait_ge(s_ri, b.ago(1).count(2, 2))
                pool.tensor_tensor(ms[:, :], ss[:, b.par, :], rms_eps[:, :], ALU.add).then_inc(s_ri, 1)
                pool.wait_ge(s_ri, b.count(2, 1))
                if not b.before(2):
                    pool.wait_ge(s_res, b.ago(2).count(NT, NT))
                pool.tensor_tensor(rinv[:, b.par, :], ms[:, :], pow_half[:, 0:NT], ALU.pow).then_inc(s_ri, 1)

            def inv_std(b):
                pool.wait_ge(s_mv, b.count(NT, NT))
                if not b.before(1):
                    pool.wait_ge(s_rs, b.ago(1).count(1, 1))
                pool.tensor_tensor(ve[:, :], mv[:, :, 1], ln_eps[:, :], ALU.add).then_inc(s_ve, 1)
                pool.wait_ge(s_ve, b.count(1, 1))
                if not b.before(1):
                    pool.wait_ge(s_x1, b.ago(1).count(NT, NT))
                pool.tensor_tensor(rstd[:, :], ve[:, :], pow_half[:, 0:NT], ALU.pow).then_inc(s_rs, 1)

            pool.wait_ge(s_load, 16 * N_LOADS)
            pool.wait_ge(s_pow, 4)
            x_low(Item(0, 0))

            def x_low_next(b):
                if not (b.known() and b.value() + 1 >= n_seq):
                    x_low(b.ago(-1))

            run_steps(pool, n_seq, [
                (x_low_next, 0), (inv_rms, 2), (scale_x, 1), (join, 1), (spread_l, 0), (inv_std, 2)], spare=2)


class Unit:
    PER = 8

    def __init__(self, item, v):
        self.item, self.v, self.par = item, v, v % 2

    def ago(self, n):
        back = -((self.v - n) // self.PER)
        return Unit(self.item.ago(back), (self.v - n) % self.PER)

    def before(self, n):
        return self.item.known() and self.item.value() * self.PER + self.v < n

    def count(self, per, done):
        return self.item.count(self.PER * per, self.v * per + done)


def by_unit(stages, after):
    out = []
    for v in range(Unit.PER):
        for stage, ulag, lag in stages:
            back = -((v - ulag) // Unit.PER)

            def run(b, stage=stage, w=(v - ulag) % Unit.PER):
                stage(Unit(b, w))
            out.append((run, lag + back))
        out += after.get(v, [])
    return out


class AttentionWeights:
    DH = 1024
    MH = DH // P
    CONSTANTS = 6

    def __init__(self, nc, ctx, wq, bq, wk, bk, wv, bv, wo, bo, masks):
        def sb(name, shape):
            return ctx.enter_context(nc.sbuf_tensor("b_" + name, shape, F32))

        self.sources = (wq, bq, wk, bk, wv, bv, wo, bo, masks)
        self.w_stage = sb("w_stage", [P, 3, self.MH * D])
        self.wk_f = sb("wk_f", [P, KD, self.DH])
        self.bq_c = sb("bq_c", [P, self.MH])
        self.bk_c = sb("bk_c", [P, self.MH])
        self.bv_b = sb("bv_b", [P, self.DH])
        self.bo_b = sb("bo_b", [P, D])
        self.mk = sb("mk", [P, 3, P])
        self.s_w = [ctx.enter_context(nc.semaphore(f"b_w{i}")) for i in range(3)]
        self.s_c = ctx.enter_context(nc.semaphore("b_const"))

    def load(self, sp):
        wq, bq, wk, bk, wv, bv, wo, bo, masks = self.sources
        for i, w in enumerate((wq, wv, wo)):
            sp.dma_start(self.w_stage[:, i, :].rearrange("p (k n) -> p k n", k=w.shape[0] // P),
                         w.rearrange("(k p) n -> p k n", p=P)).then_inc(self.s_w[i], 16)
        sp.dma_start(self.wk_f[:, :, :], wk.rearrange("(k p) n -> p k n", p=P)).then_inc(self.s_c, 16)
        sp.dma_start(self.bq_c[:, :], bq).then_inc(self.s_c, 16)
        sp.dma_start(self.bk_c[:, :], bk).then_inc(self.s_c, 16)
        sp.dma_start(self.bv_b[:, :], bv.partition_broadcast(P)).then_inc(self.s_c, 16)
        sp.dma_start(self.bo_b[:, :], bo.partition_broadcast(P)).then_inc(self.s_c, 16)
        sp.dma_start(self.mk[:, :, :], masks).then_inc(self.s_c, 16)


def attention_phase(nc, n_seq, x1, ctxT, x2, weights):
    LK, H, HD = 77, 16, 64
    DH = H * HD
    MH = DH // P
    G = 4
    GM = G * HD // P
    LN_EPS = 1e-5

    with ExitStack() as ctx:
        def sb(name, shape, dt=F32):
            return ctx.enter_context(nc.sbuf_tensor("b_" + name, shape, dt))

        def sem(name):
            return ctx.enter_context(nc.semaphore("b_" + name))

        w_stage, wk_f, bq_c, bk_c = weights.w_stage, weights.wk_f, weights.bq_c, weights.bk_c
        bv_b, bo_b, ident = weights.bv_b, weights.bo_b, weights.mk[:, 2, :]
        wq_hi = sb("wq_hi", [P, KD, DH], F32R)
        wq_lo = sb("wq_lo", [P, KD, DH], F32R)
        wv_hi = sb("wv_hi", [P, KD, DH], F32R)
        wv_lo = sb("wv_lo", [P, KD, DH], F32R)
        wo_hi = sb("wo_hi", [P, MH, D], F32R)
        wo_lo = sb("wo_lo", [P, MH, D], F32R)
        spare = sb("spare", [P, 1])
        pow_half = sb("pow_half", [P, 1])
        ln_eps = sb("ln_eps", [P, 1])

        xa = sb("xa", [P, 2, NT, D])
        xr = sb("xr", [P, 2, NT, D])
        xrb = sb("xrb", [P, 2, NT, D])
        xT_hi = sb("xT_hi", [P, 2, KD, L], F32R)
        xT_lo = sb("xT_lo", [P, 2, KD, L], F32R)
        c_f = sb("c_f", [P, 2, KD, LK])
        c_hi = sb("c_hi", [P, 2, KD, LK], F32R)
        c_lo = sb("c_lo", [P, 2, KD, LK], F32R)
        qT = sb("qT", [P, 2, MH, L])
        kz = sb("kz", [P, 2, MH, 2, LK])
        vv = sb("vv", [LK, 2, H, HD + 1])
        mx = sb("mx", [P, 2, G])
        sd = sb("sd", [P, 2, G, LK])
        pe_ = sb("pe_", [P, 2, G, LK])
        pT = sb("pT", [LK, 2, G, P])
        rec = sb("rec", [P, 2, G])
        o_n = sb("o_n", [P, 2, G, HD])
        oT_hi = sb("oT_hi", [P, 2, GM, P], F32R)
        oT_lo = sb("oT_lo", [P, 2, GM, P], F32R)
        res = sb("res", [P, 2, D])
        st = sb("st", [P, 2, 6])
        mv = sb("mv", [P, 2, 2])
        ve = sb("ve", [P, 2])
        rstd = sb("rstd", [P, 2])
        x2_t = sb("x2_t", [P, 2, NT, D])

        ps_s = [ctx.enter_context(nc.psum_tensor(f"b_ps_s{i}", [P, 512], F32)) for i in range(2)]
        ps_qk = ctx.enter_context(nc.psum_tensor("b_ps_qk", [P, 512], F32))
        ps_x = ctx.enter_context(nc.psum_tensor("b_ps_x", [P, 512], F32))
        ps_pT = ctx.enter_context(nc.psum_tensor("b_ps_pT", [P, 512], F32))
        ps_o = ctx.enter_context(nc.psum_tensor("b_ps_o", [P, 512], F32))
        ps_oT = ctx.enter_context(nc.psum_tensor("b_ps_oT", [P, 512], F32))
        ps_out = ctx.enter_context(nc.psum_tensor("b_ps_out", [P, 512], F32))

        s_w, s_c = weights.s_w, weights.s_c
        s_whi, s_wlo, s_zero = sem("whi"), [sem(f"wlo{i}") for i in range(3)], sem("zero")
        s_xa_in, s_xr_in, s_c_in, s_x2_out = ([sem(f"{n}{i}") for i in range(2)]
                                              for n in ("xa_in", "xr_in", "c_in", "x2_out"))
        s_x, s_qk, s_v, s_s, s_pT, s_o, s_oT, s_out = (
            sem(n) for n in ("x", "qk", "v", "s", "pT", "o", "oT", "out"))
        s_xhi, s_qkc, s_exp, s_ohi = (sem(n) for n in ("xhi", "qkc", "exp", "ohi"))
        s_pTc = [sem("pTc0"), sem("pTc1")]
        s_xlo, s_chi, s_vc, s_mx, s_sd, s_rec, s_on, s_olo, s_res, s_st, s_mv, s_x2 = (
            sem(n) for n in ("xlo", "chi", "vc", "mx", "sd", "rec", "on", "olo", "res", "st", "mv", "x2"))
        s_clo, s_xrb, s_ve, s_rs = (sem(n) for n in ("clo", "xrb", "ve", "rs"))

        block = ctx.enter_context(nc.Block())

        def half_count(u):
            return u.item.count(4, u.v // 2 + 1)

        def copy_p(eng, u):
            eng.wait_ge(s_pT, u.count(1, 1))
            if not u.before(2):
                eng.wait_ge(s_o, u.ago(2).count(1, 1))

        def split_low(eng, i, hi, lo):
            eng.wait_ge(s_whi, i + 1)
            eng.tensor_tensor(lo[:, :, :].rearrange("p k n -> p (k n)"), w_stage[:, i, :],
                              hi[:, :, :].rearrange("p k n -> p (k n)").bitcast(F32), ALU.subtract
                              ).then_inc(s_wlo[i], 1)

        @block.sync
        def _(sp):
            def rows(a, b):
                return a[bass.ds(b.value() * L, L), :].rearrange("(c p) d -> p c d", p=P)

            def load_xa(b):
                if not b.before(2):
                    sp.wait_ge(s_x, b.ago(2).count(1, 1))
                sp.dma_start(xa[:, b.par, :, :], rows(x1, b)).then_inc(s_xa_in[b.par], 16)

            def load_c(b):
                if not b.before(2):
                    sp.wait_ge(s_qk, b.ago(2).count(8, 8))
                    sp.wait_ge(s_clo, b.ago(2).count(1, 1))
                sp.dma_start(c_f[:, b.par, :, :], ctxT[:, :, bass.ds(b.value() * LK, LK)]).then_inc(s_c_in[b.par], 16)

            def load_xr(b):
                if not b.before(2):
                    sp.wait_ge(s_xrb, b.ago(2).count(1, 1))
                sp.dma_start(xr[:, b.par, :, :], rows(x1, b)).then_inc(s_xr_in[b.par], 16)

            def store(b):
                sp.wait_ge(s_x2, b.count(NT, NT))
                sp.dma_start(rows(x2, b), x2_t[:, b.par, :, :]).then_inc(s_x2_out[b.par], 16)

            def load_xa_ahead(b):
                if not (b.known() and b.value() + 1 >= n_seq):
                    load_xa(b.ago(-1))

            load_xa(Item(0, 0))
            run_steps(sp, n_seq, [(load_c, 0), (load_xa_ahead, 0), (load_xr, 1), (store, 3)], spare=2)
            for par in (0, 1):
                sp.wait_ge(s_x2_out[par], 16 * (n_seq // 2))

        @block.tensor
        def _(pe):
            pe.wait_ge(s_c, 16 * weights.CONSTANTS)

            def turn_x(b):
                pe.wait_ge(s_xa_in[b.par], b.half * 16 + 16)
                if not b.before(1):
                    pe.wait_ge(s_vc, b.ago(1).count(2, 2))
                for k in range(KD):
                    for c in range(NT):
                        last = pe.transpose(ps_x[:, L * k + P * c:L * k + P * c + P],
                                            xa[:, b.par, c, P * k:P * k + P], ident)
                last.then_inc(s_x, 1)

            def queries_keys(u):
                b, m = u.item, u.v
                if u.before(1):
                    pe.wait_ge(s_wlo[0], 1)
                if m == 0:
                    pe.wait_ge(s_xhi, b.count(1, 1))
                    pe.wait_ge(s_xlo, b.count(1, 1))
                    pe.wait_ge(s_c_in[b.par], b.half * 16 + 16)
                if not u.before(1):
                    pe.wait_ge(s_qkc, u.ago(1).count(1, 1))
                for k in range(KD):
                    split3(pe, ps_qk[:, 0:L], (wq_hi[:, k, P * m:P * m + P], wq_lo[:, k, P * m:P * m + P]),
                           (xT_hi[:, b.par, k, :], xT_lo[:, b.par, k, :]), k == 0, k == KD - 1)
                for k in range(KD):
                    last = pe.matmul(ps_qk[:, L:L + LK], wk_f[:, k, P * m:P * m + P], c_f[:, b.par, k, :],
                                     start=(k == 0), stop=(k == KD - 1))
                last.then_inc(s_qk, 1)

            def values(half):
                def run(b):
                    if b.before(1):
                        pe.wait_ge(s_wlo[1], 1)
                    pe.wait_ge(s_clo, b.count(1, 1))
                    if half:
                        pe.wait_ge(s_vc, b.count(2, 1))
                    else:
                        pe.wait_ge(s_xlo, b.count(1, 1))
                    for k in range(KD):
                        last = split3(pe, ps_x[0:LK, :], (c_hi[:, b.par, k, :], c_lo[:, b.par, k, :]),
                                      (wv_hi[:, k, 512 * half:512 * half + 512],
                                       wv_lo[:, k, 512 * half:512 * half + 512]), k == 0, k == KD - 1)
                    last.then_inc(s_v, 1)
                return run

            def scores(u):
                b, j, g = u.item, u.v // 4, u.v % 4
                pe.wait_ge(s_qkc, b.count(8, 8))
                if not u.before(2):
                    pe.wait_ge(s_sd, u.ago(2).count(1, 1))
                for i in range(GM):
                    last = pe.matmul(ps_s[u.par][:, 2 * LK * i:2 * LK * i + 2 * LK],
                                     qT[:, b.par, GM * g + i, P * j:P * j + P],
                                     kz[:, b.par, GM * g + i, :, :].rearrange("p a k -> p (a k)"),
                                     start=True, stop=True)
                last.then_inc(s_s, 1)

            def turn_p(u):
                pe.wait_ge(s_exp, u.count(1, 1))
                if not u.before(1):
                    prev = u.ago(1)
                    pe.wait_ge(s_pTc[prev.par], half_count(prev))
                for i in range(G):
                    last = pe.transpose(ps_pT[0:LK, P * i:P * i + P], pe_[:, u.par, i, :], ident)
                last.then_inc(s_pT, 1)

            def attend(u):
                b, g = u.item, u.v % 4
                pe.wait_ge(s_pTc[u.par], half_count(u))
                pe.wait_ge(s_vc, b.count(2, 2))
                if not u.before(1):
                    pe.wait_ge(s_on, u.ago(1).count(1, 1))
                for i in range(G):
                    last = pe.matmul(ps_o[:, (HD + 1) * i:(HD + 1) * i + HD + 1], pT[:, u.par, i, :],
                                     vv[:, b.par, G * g + i, :], start=True, stop=True)
                last.then_inc(s_o, 1)

            def turn_o(u):
                pe.wait_ge(s_on, u.count(1, 1))
                if not u.before(1):
                    pe.wait_ge(s_olo, u.ago(1).count(1, 1))
                flat = o_n[:, u.par, :, :].rearrange("p g d -> p (g d)")
                for i in range(GM):
                    last = pe.transpose(ps_oT[:, P * i:P * i + P], flat[:, P * i:P * i + P], ident)
                last.then_inc(s_oT, 1)

            def project(u):
                b, j, g = u.item, u.v // 4, u.v % 4
                if u.before(1):
                    pe.wait_ge(s_wlo[2], 1)
                pe.wait_ge(s_olo, u.count(1, 1))
                if g == 0 and not u.before(4):
                    pe.wait_ge(s_res, u.ago(4).item.count(NT, u.ago(4).v // 4 + 1))
                for i in range(GM):
                    last = split3(pe, ps_out[:, 0:D], (oT_hi[:, u.par, i, :], oT_lo[:, u.par, i, :]),
                                  (wo_hi[:, GM * g + i, :], wo_lo[:, GM * g + i, :]),
                                  g == 0 and i == 0, g == 3 and i == GM - 1)
                last.then_inc(s_out, 1)

            run_steps(pe, n_seq, by_unit(
                [(queries_keys, 0, 1), (scores, 0, 2), (turn_p, 1, 2), (attend, 2, 2), (turn_o, 3, 2), (project, 4, 2)],
                {0: [(values(0), 1)], 2: [(values(1), 1)], 5: [(turn_x, 0)]}))

        @block.scalar
        def _(act):
            for i, hi in enumerate((wq_hi, wv_hi, wo_hi)):
                act.wait_ge(s_w[i], 16)
                act.activation(hi[:, :, :].rearrange("p k n -> p (k n)"), w_stage[:, i, :], ACT.Copy).then_inc(s_whi, 1)
            act.wait_ge(s_c, 16 * weights.CONSTANTS)
            act.wait_ge(s_zero, 3)

            def x_high(b):
                act.wait_ge(s_x, b.count(1, 1))
                if not b.before(2):
                    act.wait_ge(s_qk, b.ago(2).count(8, 8))
                act.activation(xT_hi[:, b.par, :, :].rearrange("p k t -> p (k t)"), ps_x[:, :], ACT.Copy
                               ).then_inc(s_xhi, 1)

            def copy_qk(u):
                b, m = u.item, u.v
                act.wait_ge(s_qk, u.count(1, 1))
                if m == 0 and not b.before(2):
                    act.wait_ge(s_s, b.ago(2).count(8, 8))
                act.activation(qT[:, b.par, m, :], ps_qk[:, 0:L], ACT.Identity, bias=bq_c[:, m:m + 1])
                for i in range(2):
                    half = slice(HD * i, HD * i + HD)
                    last = act.activation(kz[half, b.par, m, i, :], ps_qk[half, L:L + LK], ACT.Identity,
                                          bias=bk_c[half, m:m + 1])
                last.then_inc(s_qkc, 1)

            def exps(u):
                act.wait_ge(s_sd, u.count(1, 1))
                if not u.before(2):
                    act.wait_ge(s_pT, u.ago(2).count(1, 1))
                act.activation(pe_[:, u.par, :, :], sd[:, u.par, :, :], ACT.Exp, scale=HD ** -0.5).then_inc(s_exp, 1)

            def copy_p_odd(u):
                if u.par == 1:
                    copy_p(act, u)
                    act.activation(pT[:, u.par, :, :].rearrange("p g q -> p (g q)"), ps_pT[0:LK, :], ACT.Copy
                                   ).then_inc(s_pTc[1], 1)

            def o_high(u):
                act.wait_ge(s_oT, u.count(1, 1))
                if not u.before(2):
                    act.wait_ge(s_out, u.ago(2).count(1, 1))
                act.activation(oT_hi[:, u.par, :, :].rearrange("p i q -> p (i q)"), ps_oT[:, 0:GM * P], ACT.Copy
                               ).then_inc(s_ohi, 1)

            run_steps(act, n_seq, by_unit(
                [(copy_qk, 0, 1), (copy_p_odd, 1, 2), (exps, 0, 2), (o_high, 3, 2)], {5: [(x_high, 0)]}))

        @block.vector
        def _(dve):
            dve.memset(kz[:, :, :, :, :], 0.0).then_inc(s_zero, 1)
            dve.memset(vv[:, :, :, :], 1.0).then_inc(s_zero, 1)
            dve.memset(pow_half[:, :], -0.5).then_inc(s_zero, 1)
            dve.memset(ln_eps[:, :], LN_EPS).then_inc(s_zero, 1)
            for i, (hi, lo) in enumerate(((wq_hi, wq_lo), (wv_hi, wv_lo))):
                split_low(dve, i, hi, lo)
            dve.wait_ge(s_c, 16 * weights.CONSTANTS)
            dve.wait_ge(s_zero, 3)

            def x_low(b):
                dve.wait_ge(s_xhi, b.count(1, 1))
                dve.tensor_tensor(xT_lo[:, b.par, :, :].rearrange("p k t -> p (k t)"), ps_x[:, :],
                                  xT_hi[:, b.par, :, :].rearrange("p k t -> p (k t)").bitcast(F32), ALU.subtract
                                  ).then_inc(s_xlo, 1)

            def c_high(b):
                dve.wait_ge(s_c_in[b.par], b.half * 16 + 16)
                if not b.before(2):
                    dve.wait_ge(s_v, b.ago(2).count(2, 2))
                dve.tensor_copy(c_hi[:, b.par, :, :], c_f[:, b.par, :, :]).then_inc(s_chi, 1)

            def copy_v(half):
                def run(b):
                    dve.wait_ge(s_v, b.count(2, half + 1))
                    if not b.before(2):
                        dve.wait_ge(s_o, b.ago(2).count(8, 8))
                    dve.tensor_tensor(vv[:, b.par, 8 * half:8 * half + 8, 0:HD],
                                      ps_x[0:LK, :].rearrange("p (h d) -> p h d", h=8),
                                      bv_b[0:LK, 512 * half:512 * half + 512].rearrange("p (h d) -> p h d", h=8),
                                      ALU.add).then_inc(s_vc, 1)
                return run

            def subtract_max(u):
                dve.wait_ge(s_s, u.count(1, 1))
                s = ps_s[u.par][:, 0:G * LK].rearrange("p (g k) -> p g k", g=G)
                dve.tensor_reduce(mx[:, u.par, :], s, AX.X, ALU.max).then_inc(s_mx, 1)
                dve.wait_ge(s_mx, u.count(1, 1))
                if not u.before(2):
                    dve.wait_ge(s_exp, u.ago(2).count(1, 1))
                dve.tensor_tensor(sd[:, u.par, :, :], s, mx[:, u.par, :].unsqueeze(2).to_broadcast([P, G, LK]),
                                  ALU.subtract).then_inc(s_sd, 1)

            def copy_p_even(u):
                if u.par == 0:
                    copy_p(dve, u)
                    dve.tensor_copy(pT[:, u.par, :, :].rearrange("p g q -> p (g q)"), ps_pT[0:LK, :]
                                    ).then_inc(s_pTc[0], 1)

            def divide(u):
                dve.wait_ge(s_o, u.count(1, 1))
                o = ps_o[:, 0:G * (HD + 1)].rearrange("p (g d) -> p g d", g=G)
                dve.reciprocal(rec[:, u.par, :], o[:, :, HD]).then_inc(s_rec, 1)
                dve.wait_ge(s_rec, u.count(1, 1))
                if not u.before(2):
                    dve.wait_ge(s_oT, u.ago(2).count(1, 1))
                dve.tensor_tensor(o_n[:, u.par, :, :], o[:, :, 0:HD],
                                  rec[:, u.par, :].unsqueeze(2).to_broadcast([P, G, HD]), ALU.mult).then_inc(s_on, 1)

            def o_low(u):
                dve.wait_ge(s_ohi, u.count(1, 1))
                dve.tensor_tensor(oT_lo[:, u.par, :, :].rearrange("p i q -> p (i q)"), ps_oT[:, 0:GM * P],
                                  oT_hi[:, u.par, :, :].rearrange("p i q -> p (i q)").bitcast(F32), ALU.subtract
                                  ).then_inc(s_olo, 1)

            def residual(u):
                if u.v % 4 != 3:
                    return
                b, j = u.item, u.v // 4
                dve.wait_ge(s_out, u.count(1, 1))
                if j == 0:
                    dve.wait_ge(s_xrb, b.count(1, 1))
                if not b.before(1):
                    dve.wait_ge(s_x2, b.ago(1).count(NT, j + 1))
                dve.tensor_tensor(res[:, j, :], ps_out[:, 0:D], xrb[:, b.par, j, :], ALU.add).then_inc(s_res, 1)
                dve.wait_ge(s_res, b.count(NT, j + 1))
                dve.bn_stats(st[:, j, :], res[:, j, :]).then_inc(s_st, 1)
                wait_apart(dve, spare[0:1, :], (s_st, b.count(NT, j + 1)))
                dve.bn_aggr(mv[:, j, :], st[:, j, :]).then_inc(s_mv, 1)

            def normalise(u):
                if u.v % 4 != 3:
                    return
                b, j = u.item, u.v // 4
                dve.wait_ge(s_rs, b.count(NT, j + 1))
                if not b.before(2):
                    dve.wait_ge(s_x2_out[b.par], b.half * 16)
                dve.tensor_scalar(x2_t[:, b.par, j, :], res[:, j, :], mv[:, j, 0:1], rstd[:, j:j + 1],
                                  ALU.subtract, ALU.mult).then_inc(s_x2, 1)

            run_steps(dve, n_seq, by_unit(
                [(subtract_max, 0, 2), (copy_p_even, 1, 2), (divide, 2, 2), (o_low, 3, 2), (residual, 4, 2),
                 (normalise, 5, 2)],
                {0: [(copy_v(0), 1)], 2: [(copy_v(1), 1)], 5: [(x_low, 0), (c_high, 0)]}))

        @block.gpsimd
        def _(pool):
            pool.wait_ge(s_c, 16 * weights.CONSTANTS)
            pool.wait_ge(s_zero, 4)

            def c_low(b):
                pool.wait_ge(s_chi, b.count(1, 1))
                if not b.before(2):
                    pool.wait_ge(s_v, b.ago(2).count(2, 2))
                pool.tensor_tensor(c_lo[:, b.par, :, :], c_f[:, b.par, :, :], c_hi[:, b.par, :, :].bitcast(F32),
                                   ALU.subtract).then_inc(s_clo, 1)

            def add_bo(b):
                pool.wait_ge(s_xr_in[b.par], b.half * 16 + 16)
                if not b.before(2):
                    pool.wait_ge(s_res, b.ago(2).count(NT, NT))
                pool.tensor_tensor(xrb[:, b.par, :, :], xr[:, b.par, :, :],
                                   bo_b[:, :].unsqueeze(1).to_broadcast([P, NT, D]), ALU.add).then_inc(s_xrb, 1)

            def inv_std(u):
                if u.v % 4 != 3:
                    return
                b, j = u.item, u.v // 4
                pool.wait_ge(s_mv, b.count(NT, j + 1))
                pool.tensor_tensor(ve[:, j:j + 1], mv[:, j, 1:2], ln_eps[:, :], ALU.add).then_inc(s_ve, 1)
                pool.wait_ge(s_ve, b.count(NT, j + 1))
                if not b.before(1):
                    pool.wait_ge(s_x2, b.ago(1).count(NT, j + 1))
                pool.tensor_tensor(rstd[:, j:j + 1], ve[:, j:j + 1], pow_half[:, :], ALU.pow).then_inc(s_rs, 1)

            c_low(Item(0, 0))
            split_low(pool, 2, wo_hi, wo_lo)

            def c_low_later(b):
                if not b.before(1):
                    c_low(b)

            run_steps(pool, n_seq, by_unit([(inv_std, 4, 2)], {5: [(c_low_later, 0), (add_bo, 1)]}))


def experts_phase(nc, n_seq, x2, out, gate_w, w1, b1, w2, b2, ln_g, ln_b, masks):
    E, F = 8, 512
    MF = F // P
    LN_E, LN_EPS = 1e-6, 1e-5
    SLOTS = 3
    assert E == Unit.PER

    with ExitStack() as ctx:
        def sb(name, shape, dt=F32):
            return ctx.enter_context(nc.sbuf_tensor("c_" + name, shape, dt))

        def sem(name):
            return ctx.enter_context(nc.semaphore("c_" + name))

        stage = sb("stage", [P, SLOTS, 2 * F])
        gw = sb("gw", [P, KD, E])
        b1_c = sb("b1_c", [P, E, MF])
        b2_b = sb("b2_b", [P, E, D])
        g_b = sb("g_b", [P, E, D])
        lnb = sb("lnb", [E, D])
        ident = sb("ident", [P, P])
        w1_hi = sb("w1_hi", [P, E, KD, F], F32R)
        w1_lo = sb("w1_lo", [P, E, KD, F], F32R)
        w2_hi = sb("w2_hi", [P, E, MF, D], F32R)
        w2_lo = sb("w2_lo", [P, E, MF, D], F32R)
        spare = sb("spare", [P, 1])
        pow_half = sb("pow_half", [P, NT])
        ln_e_eps = sb("ln_e_eps", [P, NT])
        ln_eps = sb("ln_eps", [P, NT])
        euler = sb("euler", [P, NT])
        iota_e = sb("iota_e", [P, E])

        xa = sb("xa", [P, 2, NT, D])
        xT_f = sb("xT_f", [P, KD, L])
        xT_hi = sb("xT_hi", [P, 2, KD, L], F32R)
        xT_lo = sb("xT_lo", [P, 2, KD, L], F32R)
        hid = sb("hid", [P, MF * L])
        h_hi = sb("h_hi", [P, 2, MF * L], F32R)
        h_lo = sb("h_lo", [P, 2, MF * L], F32R)
        sg = sb("sg", [P, NT, E])
        top = sb("top", [P, NT, 8])
        idx = sb("idx", [P, NT, 8], U32)
        idx_f = sb("idx_f", [P, NT, 2])
        gap = sb("gap", [P, NT])
        e2 = sb("e2", [P, NT])
        e2p = sb("e2p", [P, NT])
        wt = sb("wt", [P, NT, 2])
        pick = sb("pick", [P, NT, 2, E])
        wE = sb("wE", [P, 2, NT, E])
        wET = sb("wET", [E, L])
        xb = sb("xb", [P, 2, NT, D])
        yy = sb("yy", [P, NT, D])
        st = sb("st", [P, NT, 6])
        mv = sb("mv", [P, 2, NT, 2])
        ve = sb("ve", [P, NT])
        rs = sb("rs", [P, NT])
        sc = sb("sc", [P, 2, NT])
        tt = sb("tt", [P, 2, NT, D])
        acc = sb("acc", [P, 2, NT, D])
        fst = sb("fst", [P, NT, 6])
        fmv = sb("fmv", [P, NT, 2])
        fve = sb("fve", [P, NT])
        frs = sb("frs", [P, NT])

        ps_h = [ctx.enter_context(nc.psum_tensor(f"c_ps_h{i}", [P, 2, 512], F32)) for i in range(2)]
        ps_o = [ctx.enter_context(nc.psum_tensor(f"c_ps_o{i}", [P, 512], F32)) for i in range(2)]
        ps_x = ctx.enter_context(nc.psum_tensor("c_ps_x", [P, 512], F32))
        ps_g = ctx.enter_context(nc.psum_tensor("c_ps_g", [P, 512], F32))

        s_w = [sem(f"weights{i}") for i in range(SLOTS)]
        s_c, s_bg, s_one = sem("const"), sem("bg"), sem("one")
        s_whi, s_w1lo, s_w2lo = sem("whi"), sem("w1lo"), sem("w2lo")
        s_xa_in = [sem(f"xa_in{i}") for i in range(2)]
        s_o_out = sem("o_out")
        s_x, s_g, s_wt, s_wb, s_h, s_o = (sem(n) for n in ("x", "g", "wt", "wb", "h", "o"))
        s_xf, s_e2, s_gelu, s_hhi, s_wtc = (sem(n) for n in ("xf", "e2", "gelu", "hhi", "wtc"))
        s_xhi, s_sg, s_top, s_idx, s_if, s_gap, s_p1r, s_w2, s_pick, s_wE = (
            sem(n) for n in ("xhi", "sg", "top", "idx", "if", "gap", "p1r", "w2", "pick", "wE"))
        s_hlo, s_y, s_st, s_mv, s_t, s_a0, s_acc, s_fst, s_fmv, s_fo = (
            sem(n) for n in ("hlo", "y", "st", "mv", "t", "a0", "acc", "fst", "fmv", "fo"))
        s_xlo, s_xb, s_ve, s_rs, s_sc, s_frs = (
            sem(n) for n in ("xlo", "xb", "ve", "rs", "sc", "frs"))

        block = ctx.enter_context(nc.Block())

        def rows(a, b):
            return a[bass.ds(b.value() * L, L), :].rearrange("(c p) d -> p c d", p=P)

        @block.sync
        def _(sp):
            def load_weights(n):
                w = (w1, w2)[n % 2][n // 2]
                sp.dma_start(stage[:, n % SLOTS, :].rearrange("p (k n) -> p k n", k=(KD, MF)[n % 2]),
                             w.rearrange("(k p) n -> p k n", p=P)).then_inc(s_w[n % SLOTS], 16)

            sp.dma_start(xa[:, 0, :, :], rows(x2, Item(0, 0))).then_inc(s_xa_in[0], 16)
            sp.dma_start(ident[:, :], masks[:, 2, :]).then_inc(s_c, 16)
            sp.dma_start(gw[:, :, :], gate_w.rearrange("(k p) e -> p k e", p=P)).then_inc(s_c, 16)
            load_weights(0)
            sp.dma_start(b1_c[:, :, :], b1).then_inc(s_c, 16)
            sp.dma_start(lnb[:, :], ln_b).then_inc(s_c, 16)
            load_weights(1)
            load_weights(2)
            sp.dma_start(xa[:, 1, :, :], rows(x2, Item(0, 1))).then_inc(s_xa_in[1], 16)
            sp.dma_start(b2_b[:, :, :], b2.partition_broadcast(P)).then_inc(s_bg, 16)
            sp.dma_start(g_b[:, :, :], ln_g.partition_broadcast(P)).then_inc(s_bg, 16)
            for n in range(SLOTS, 2 * E):
                old_e, old_j = divmod(n - SLOTS, 2)
                sp.wait_ge((s_w1lo, s_w2lo)[old_j], old_e + 1)
                load_weights(n)

            def load(b):
                if not b.before(2):
                    sp.wait_ge(s_xb, b.ago(2).count(E, E))
                sp.dma_start(xa[:, b.par, :, :], rows(x2, b)).then_inc(s_xa_in[b.par], 16)

            def load_ahead(b):
                if not b.before(1) and not (b.known() and b.value() + 1 >= n_seq):
                    load(b.ago(-1))

            def store(b):
                sp.wait_ge(s_fo, b.count(NT, NT))
                sp.dma_start(rows(out, b), acc[:, b.par, :, :]).then_inc(s_o_out, 16)

            run_steps(sp, n_seq, [(load_ahead, 1), (store, 2)])
            sp.wait_ge(s_o_out, 16 * n_seq)

        @block.tensor
        def _(pe):
            pe.wait_ge(s_c, 16 * 4)

            def turn_x(b):
                pe.wait_ge(s_xa_in[b.par], b.half * 16 + 16)
                if not b.before(1):
                    pe.wait_ge(s_xhi, b.ago(1).count(1, 1))
                for k in range(KD):
                    for c in range(NT):
                        last = pe.transpose(ps_x[:, L * k + P * c:L * k + P * c + P],
                                            xa[:, b.par, c, P * k:P * k + P], ident[:, :])
                last.then_inc(s_x, 1)

            def gate(b):
                pe.wait_ge(s_xf, b.count(1, 1))
                if not b.before(1):
                    pe.wait_ge(s_a0, b.ago(1).count(NT, NT))
                for c in range(NT):
                    for k in range(KD):
                        last = pe.matmul(ps_g[:, E * c:E * c + E], xT_f[:, k, P * c:P * c + P], gw[:, k, :],
                                         start=(k == 0), stop=(k == KD - 1))
                last.then_inc(s_g, 1)

            def turn_w(b):
                pe.wait_ge(s_wE, b.count(1, 1))
                for c in range(NT):
                    last = pe.transpose(ps_g[0:E, P * c:P * c + P], wE[:, b.par, c, :], ident[:, :])
                last.then_inc(s_wt, 1)

            def bias_w(b):
                pe.wait_ge(s_wtc, b.count(1, 1))
                for c in range(NT):
                    last = pe.matmul(ps_g[:, D * c:D * c + D], wET[:, P * c:P * c + P], lnb[:, :],
                                     start=True, stop=True)
                last.then_inc(s_wb, 1)

            def up(u):
                b, e = u.item, u.v
                if e == 0:
                    pe.wait_ge(s_xhi, b.count(1, 1))
                    pe.wait_ge(s_xlo, b.count(1, 1))
                if b.before(1):
                    pe.wait_ge(s_w1lo, e + 1)
                if not u.before(2):
                    pe.wait_ge(s_gelu, u.ago(2).count(1, 1))
                for m in range(MF):
                    for k in range(KD):
                        last = split3(pe, ps_h[u.par][:, m // 2, L * (m % 2):L * (m % 2) + L],
                                      (w1_hi[:, e, k, P * m:P * m + P], w1_lo[:, e, k, P * m:P * m + P]),
                                      (xT_hi[:, b.par, k, :], xT_lo[:, b.par, k, :]), k == 0, k == KD - 1)
                last.then_inc(s_h, 1)

            def down(u):
                b, e = u.item, u.v
                if b.before(1):
                    pe.wait_ge(s_w2lo, e + 1)
                pe.wait_ge(s_hlo, u.count(1, 1))
                if not u.before(2):
                    pe.wait_ge(s_y, u.ago(2).count(NT, NT))
                for c in range(NT):
                    for m in range(MF):
                        at = slice(L * m + P * c, L * m + P * c + P)
                        last = split3(pe, ps_o[u.par][:, D * c:D * c + D], (h_hi[:, u.par, at], h_lo[:, u.par, at]),
                                      (w2_hi[:, e, m, :], w2_lo[:, e, m, :]), m == 0, m == MF - 1)
                last.then_inc(s_o, 1)

            run_steps(pe, n_seq, by_unit([(up, 0, 1), (down, 1, 1)],
                                         {0: [(turn_x, 0), (turn_w, 1)], 1: [(bias_w, 1)], 3: [(gate, 0)]}))

        @block.scalar
        def _(act):
            act.wait_ge(s_c, 16 * 4)

            def x_full(b):
                act.wait_ge(s_x, b.count(1, 1))
                if not b.before(1):
                    act.wait_ge(s_g, b.ago(1).count(1, 1))
                    act.wait_ge(s_xlo, b.ago(1).count(1, 1))
                    act.wait_ge(s_xhi, b.ago(1).count(1, 1))
                act.activation(xT_f[:, :, :].rearrange("p k t -> p (k t)"), ps_x[:, :], ACT.Copy).then_inc(s_xf, 1)

            def copy_w(b):
                act.wait_ge(s_wt, b.count(1, 1))
                if not b.before(1):
                    act.wait_ge(s_wb, b.ago(1).count(1, 1))
                act.activation(wET[:, :], ps_g[0:E, 0:L], ACT.Copy).then_inc(s_wtc, 1)

            def high_w_once(u):
                if u.before(E):
                    for j, hi in enumerate((w1_hi, w2_hi)):
                        n = 2 * u.v + j
                        act.wait_ge(s_w[n % SLOTS], 16 * (n // SLOTS) + 16)
                        act.activation(hi[:, u.v, :, :].rearrange("p k n -> p (k n)"), stage[:, n % SLOTS, :], ACT.Copy
                                       ).then_inc(s_whi, 1)

            def gelu(u):
                act.wait_ge(s_h, u.count(1, 1))
                if not u.before(1):
                    act.wait_ge(s_hlo, u.ago(1).count(1, 1))
                    act.wait_ge(s_hhi, u.ago(1).count(1, 1))
                for m in range(MF):
                    last = act.activation(hid[:, L * m:L * m + L],
                                          ps_h[u.par][:, m // 2, L * (m % 2):L * (m % 2) + L], ACT.Gelu,
                                          bias=b1_c[:, u.v, m:m + 1])
                last.then_inc(s_gelu, 1)

            def h_high(u):
                act.wait_ge(s_gelu, u.count(1, 1))
                if not u.before(2):
                    act.wait_ge(s_o, u.ago(2).count(1, 1))
                act.activation(h_hi[:, u.par, :], hid[:, :], ACT.Copy).then_inc(s_hhi, 1)

            run_steps(act, n_seq, by_unit([(high_w_once, -2, 1), (gelu, 0, 1), (h_high, 0, 1)],
                                          {0: [(x_full, 0), (copy_w, 1)]}))

        @block.vector
        def _(dve):
            dve.memset(pow_half[:, :], -0.5).then_inc(s_one, 1)
            dve.memset(ln_e_eps[:, :], LN_E).then_inc(s_one, 1)
            dve.memset(ln_eps[:, :], LN_EPS).then_inc(s_one, 1)
            dve.memset(euler[:, :], math.e).then_inc(s_one, 1)

            def split_w1(e):
                dve.wait_ge(s_whi, 2 * e + 1)
                dve.tensor_tensor(w1_lo[:, e, :, :].rearrange("p k n -> p (k n)"), stage[:, 2 * e % SLOTS, :],
                                  w1_hi[:, e, :, :].rearrange("p k n -> p (k n)").bitcast(F32), ALU.subtract
                                  ).then_inc(s_w1lo, 1)

            dve.wait_ge(s_one, 5)

            def x_high(b):
                dve.wait_ge(s_xf, b.count(1, 1))
                if not b.before(2):
                    dve.wait_ge(s_h, b.ago(2).count(E, E))
                dve.tensor_copy(xT_hi[:, b.par, :, :], xT_f[:, :, :]).then_inc(s_xhi, 1)

            def route(b):
                dve.wait_ge(s_g, b.count(1, 1))
                if not b.before(1):
                    dve.wait_ge(s_idx, b.ago(1).count(NT, NT))
                    dve.wait_ge(s_gap, b.ago(1).count(1, 1))
                dve.tensor_copy(sg[:, :, :].rearrange("p c e -> p (c e)"), ps_g[:, 0:NT * E]).then_inc(s_sg, 1)
                wait_apart(dve, spare[0:1, :], (s_sg, b.count(1, 1)))
                for c in range(NT):
                    dve.max(top[:, c, :], sg[:, c, :]).then_inc(s_top, 1)
                free = [] if b.before(1) else [(s_if, b.ago(1).count(1, 1))]
                wait_apart(dve, spare[0:1, :], (s_top, b.count(NT, NT)), *free)
                for c in range(NT):
                    dve.max_index(idx[:, c, :], top[:, c, :], sg[:, c, :]).then_inc(s_idx, 1)
                if not b.before(1):
                    dve.wait_ge(s_e2, b.ago(1).count(1, 1))
                dve.tensor_tensor(gap[:, :], top[:, :, 1], top[:, :, 0], ALU.subtract).then_inc(s_gap, 1)
                dve.wait_ge(s_idx, b.count(NT, NT))
                if not b.before(1):
                    dve.wait_ge(s_pick, b.ago(1).count(2 * NT, 2 * NT))
                dve.tensor_copy(idx_f[:, :, :], idx[:, :, 0:2]).then_inc(s_if, 1)

            def softmax_top(b):
                dve.wait_ge(s_e2, b.count(1, 1))
                dve.tensor_scalar(e2p[:, :], e2[:, :], 1.0, None, ALU.add).then_inc(s_p1r, 1)
                dve.wait_ge(s_p1r, b.count(2, 1))
                if not b.before(1):
                    dve.wait_ge(s_pick, b.ago(1).count(2 * NT, 2 * NT))
                dve.reciprocal(wt[:, :, 0], e2p[:, :]).then_inc(s_p1r, 1)
                dve.wait_ge(s_p1r, b.count(2, 2))
                dve.tensor_tensor(wt[:, :, 1], e2[:, :], wt[:, :, 0], ALU.mult).then_inc(s_w2, 1)
                dve.wait_ge(s_if, b.count(1, 1))
                dve.wait_ge(s_w2, b.count(1, 1))
                if not b.before(1):
                    dve.wait_ge(s_wE, b.ago(1).count(1, 1))
                for c in range(NT):
                    for n in range(2):
                        dve.tensor_scalar(pick[:, c, n, :], iota_e[:, :], idx_f[:, c, n:n + 1], wt[:, c, n:n + 1],
                                          ALU.is_equal, ALU.mult).then_inc(s_pick, 1)
                dve.wait_ge(s_pick, b.count(2 * NT, 2 * NT))
                if not b.before(2):
                    dve.wait_ge(s_sc, b.ago(2).count(E, E))
                    dve.wait_ge(s_wt, b.ago(2).count(1, 1))
                dve.tensor_tensor(wE[:, b.par, :, :], pick[:, :, 0, :], pick[:, :, 1, :], ALU.add).then_inc(s_wE, 1)

            def start_acc(b):
                dve.wait_ge(s_wb, b.count(1, 1))
                if not b.before(2):
                    dve.wait_ge(s_o_out, b.ago(2).count(16, 16))
                for c in range(NT):
                    dve.tensor_tensor(acc[:, b.par, c, :], ps_g[:, D * c:D * c + D], xa[:, b.par, c, :], ALU.add
                                      ).then_inc(s_a0, 1)

            def h_low(u):
                dve.wait_ge(s_hhi, u.count(1, 1))
                if not u.before(2):
                    dve.wait_ge(s_o, u.ago(2).count(1, 1))
                dve.tensor_tensor(h_lo[:, u.par, :], hid[:, :], h_hi[:, u.par, :].bitcast(F32), ALU.subtract
                                  ).then_inc(s_hlo, 1)

            def centre(u):
                dve.wait_ge(s_o, u.count(1, 1))
                dve.wait_ge(s_xb, u.count(1, 1))
                if not u.before(1):
                    dve.wait_ge(s_t, u.ago(1).count(NT, NT))
                for c in range(NT):
                    dve.tensor_tensor(yy[:, c, :], ps_o[u.par][:, D * c:D * c + D], xb[:, u.par, c, :], ALU.add
                                      ).then_inc(s_y, 1)
                for c in range(NT):
                    dve.wait_ge(s_y, u.count(NT, c + 1))
                    dve.bn_stats(st[:, c, :], yy[:, c, :]).then_inc(s_st, 1)
                free = [] if u.before(2) else [(s_ve, u.ago(2).count(1, 1))]
                wait_apart(dve, spare[0:1, :], (s_st, u.count(NT, NT)), *free)
                for c in range(NT):
                    dve.bn_aggr(mv[:, u.par, c, :], st[:, c, :]).then_inc(s_mv, 1)
                if not u.before(2):
                    dve.wait_ge(s_acc, u.ago(2).count(NT, NT))
                if u.before(1):
                    dve.wait_ge(s_bg, 16 * 2)
                for c in range(NT):
                    dve.wait_ge(s_mv, u.count(NT, c + 1))
                    dve.scalar_tensor_tensor(out=tt[:, u.par, c, :], in0=yy[:, c, :], scalar=mv[:, u.par, c, 0:1],
                                             in1=g_b[:, u.v, :], op0=ALU.subtract, op1=ALU.mult).then_inc(s_t, 1)

            def add_up(u):
                b = u.item
                dve.wait_ge(s_sc, u.count(1, 1))
                if u.v == 0:
                    dve.wait_ge(s_a0, b.count(NT, NT))
                for c in range(NT):
                    if u.v:
                        dve.wait_ge(s_acc, u.ago(1).count(NT, c + 1))
                    dve.scalar_tensor_tensor(out=acc[:, b.par, c, :], in0=tt[:, u.par, c, :],
                                             scalar=sc[:, u.par, c:c + 1], in1=acc[:, b.par, c, :],
                                             op0=ALU.mult, op1=ALU.add).then_inc(s_acc, 1)

            def finish(b):
                dve.wait_ge(s_acc, b.count(E * NT, E * NT))
                for c in range(NT):
                    dve.bn_stats(fst[:, c, :], acc[:, b.par, c, :]).then_inc(s_fst, 1)
                free = [] if b.before(1) else [(s_frs, b.ago(1).count(2, 1))]
                wait_apart(dve, spare[0:1, :], (s_fst, b.count(NT, NT)), *free)
                for c in range(NT):
                    dve.bn_aggr(fmv[:, c, :], fst[:, c, :]).then_inc(s_fmv, 1)

            def normalise(b):
                dve.wait_ge(s_frs, b.count(2, 2))
                for c in range(NT):
                    dve.tensor_scalar(acc[:, b.par, c, :], acc[:, b.par, c, :], fmv[:, c, 0:1], frs[:, c:c + 1],
                                      ALU.subtract, ALU.mult).then_inc(s_fo, 1)

            def split_w1_once(u):
                if u.before(E):
                    split_w1(u.v)

            run_steps(dve, n_seq, by_unit([(split_w1_once, -2, 1), (h_low, 0, 1), (centre, 1, 1), (add_up, 2, 1)],
                                          {1: [(x_high, 0), (finish, 2), (start_acc, 1)], 2: [(normalise, 2)],
                                           4: [(route, 0)], 6: [(softmax_top, 0)]}))

        @block.gpsimd
        def _(pool):
            for e in range(E):
                last = pool.memset(iota_e[:, e:e + 1], float(e))
            last.then_inc(s_one, 1)
            pool.wait_ge(s_one, 5)

            def x_low(b):
                pool.wait_ge(s_xhi, b.count(1, 1))
                if not b.before(2):
                    pool.wait_ge(s_h, b.ago(2).count(E, E))
                pool.tensor_tensor(xT_lo[:, b.par, :, :], xT_f[:, :, :], xT_hi[:, b.par, :, :].bitcast(F32),
                                   ALU.subtract).then_inc(s_xlo, 1)

            def split_w2_once(u):
                if u.before(E):
                    pool.wait_ge(s_whi, 2 * u.v + 2)
                    pool.tensor_tensor(w2_lo[:, u.v, :, :].rearrange("p k n -> p (k n)"),
                                       stage[:, (2 * u.v + 1) % SLOTS, :],
                                       w2_hi[:, u.v, :, :].rearrange("p k n -> p (k n)").bitcast(F32), ALU.subtract
                                       ).then_inc(s_w2lo, 1)

            def add_b2(u):
                b = u.item
                if u.before(1):
                    pool.wait_ge(s_bg, 16 * 2)
                if u.v == 0:
                    pool.wait_ge(s_xa_in[b.par], b.half * 16 + 16)
                if not u.before(2):
                    pool.wait_ge(s_y, u.ago(2).count(NT, NT))
                pool.tensor_tensor(xb[:, u.par, :, :], xa[:, b.par, :, :],
                                   b2_b[:, u.v, :].unsqueeze(1).to_broadcast([P, NT, D]), ALU.add).then_inc(s_xb, 1)

            def scale(u):
                b = u.item
                pool.wait_ge(s_mv, u.count(NT, NT))
                pool.wait_ge(s_wE, b.count(1, 1))
                if not u.before(1):
                    pool.wait_ge(s_rs, u.ago(1).count(1, 1))
                pool.tensor_tensor(ve[:, :], mv[:, u.par, :, 1], ln_e_eps[:, :], ALU.add).then_inc(s_ve, 1)
                pool.wait_ge(s_ve, u.count(1, 1))
                if not u.before(1):
                    pool.wait_ge(s_sc, u.ago(1).count(1, 1))
                pool.tensor_tensor(rs[:, :], ve[:, :], pow_half[:, :], ALU.pow).then_inc(s_rs, 1)
                pool.wait_ge(s_rs, u.count(1, 1))
                if not u.before(2):
                    pool.wait_ge(s_acc, u.ago(2).count(NT, NT))
                pool.tensor_tensor(sc[:, u.par, :], rs[:, :], wE[:, b.par, :, u.v], ALU.mult).then_inc(s_sc, 1)

            def exp_gap(b):
                pool.wait_ge(s_gap, b.count(1, 1))
                if not b.before(1):
                    pool.wait_ge(s_w2, b.ago(1).count(1, 1))
                pool.tensor_tensor(e2[:, :], euler[:, :], gap[:, :], ALU.pow).then_inc(s_e2, 1)

            def inv_std(b):
                pool.wait_ge(s_fmv, b.count(NT, NT))
                if not b.before(1):
                    pool.wait_ge(s_frs, b.ago(1).count(2, 2))
                pool.tensor_tensor(fve[:, :], fmv[:, :, 1], ln_eps[:, :], ALU.add).then_inc(s_frs, 1)
                pool.wait_ge(s_frs, b.count(2, 1))
                if not b.before(1):
                    pool.wait_ge(s_fo, b.ago(1).count(NT, NT))
                pool.tensor_tensor(frs[:, :], fve[:, :], pow_half[:, :], ALU.pow).then_inc(s_frs, 1)

            run_steps(pool, n_seq, by_unit([(split_w2_once, -2, 1), (add_b2, 0, 1), (scale, 1, 1)],
                                           {1: [(x_low, 0), (inv_std, 2)], 5: [(exp_gap, 0)]}))


def program(nc, n_seq, xT, x, ctxT, a_w_in, a_w_out, a_norm_w, a_conv_w, a_conv_b, a_A_log, a_D_param, a_dt_bias,
            b_wq, b_bq, b_wk, b_bk, b_wv, b_bv, b_wo, b_bo, c_gate_w, c_w1, c_b1, c_w2, c_b2, c_ln_g, c_ln_b,
            masks, out):
    x1 = nc.dram_tensor("x1_scratch", [n_seq * L, D], F32).ap()
    x2 = nc.dram_tensor("x2_scratch", [n_seq * L, D], F32).ap()
    with ExitStack() as during_ab:
        b_weights = AttentionWeights(nc, during_ab, b_wq, b_bq, b_wk, b_bk, b_wv, b_bv, b_wo, b_bo, masks)
        mixer_phase(nc, n_seq, b_weights, xT, x, x1, a_w_in, a_w_out, a_norm_w, a_conv_w, a_conv_b, a_A_log,
                    a_D_param, a_dt_bias, masks)
        attention_phase(nc, n_seq, x1, ctxT, x2, b_weights)
    experts_phase(nc, n_seq, x2, out, c_gate_w, c_w1, c_b1, c_w2, c_b2, c_ln_g, c_ln_b, masks)


def layouts(inputs):
    c = np.ascontiguousarray
    a = {k: np.asarray(v) for k, v in inputs.items()}

    def turned(m):
        return c(m.reshape(-1, KD, P).transpose(2, 1, 0))

    def columns(v):
        return c(np.moveaxis(v.reshape(*v.shape[:-1], -1, P), -1, 0))

    x = a["x"].reshape(-1, D)
    w = a["L0_attn_in_proj_w"].T
    di, h, n = 512, 8, 64
    z, xc, dt, b_, c_ = np.split(w, [di, 2 * di, 2 * di + h, 2 * di + h + n], axis=1)
    row, col = np.arange(P)[:, None], np.arange(P)[None, :]
    at, xat, ffn = ({k[len(p):]: v for k, v in a.items() if k.startswith(p)} for p in
                    ("L0_attn_", "L0_xattn_", "L0_ffn_"))
    return {
        "xT": turned(x), "x": c(x), "ctxT": turned(a["ctx_1024"].reshape(-1, D)),
        "a_w_in": c(np.concatenate([z, xc, b_, c_, c_, b_, dt], axis=1)),
        "a_w_out": c(at["out_proj_w"].T), "a_norm_w": columns(at["norm_w"]),
        "a_conv_w": c(at["conv_w"].reshape(-1, P, 4).transpose(1, 0, 2)), "a_conv_b": columns(at["conv_b"]),
        "a_A_log": at["A_log"], "a_D_param": at["D_param"], "a_dt_bias": at["dt_bias"],
        "b_wq": c(xat["Wq"].T), "b_bq": columns(xat["bq"]), "b_wk": c(xat["Wk"].T), "b_bk": columns(xat["bk"]),
        "b_wv": c(xat["Wv"].T), "b_bv": xat["bv"], "b_wo": c(xat["Wo"].T), "b_bo": xat["bo"],
        "c_gate_w": ffn["gate_w"], "c_w1": ffn["w1"], "c_b1": columns(ffn["b1"]), "c_w2": ffn["w2"],
        "c_b2": ffn["b2"], "c_ln_g": ffn["ln_g"], "c_ln_b": ffn["ln_b"],
        "masks": np.stack([row <= col, row > col, row == col], axis=1).astype(np.float32),
    }


def kernel(**inputs):
    import concourse.bacc as bacc
    from concourse.bass_utils import run_bass_kernel_spmd

    nc = bacc.Bacc("TRN2", target_bir_lowering=False, num_devices=1)
    shape = inputs["x"].shape
    arrays = layouts(inputs)
    aps = {k: nc.dram_tensor(f"in_{k}", v.shape, mybir.dt.from_np(v.dtype), kind="ExternalInput").ap()
           for k, v in arrays.items()}
    out = nc.dram_tensor("out_0", (shape[0] * shape[1], shape[2]), F32, kind="ExternalOutput").ap()
    program(nc, shape[0], out=out, **aps)
    r = run_bass_kernel_spmd(nc, [{f"in_{k}": v for k, v in arrays.items()}], core_ids=[0])
    return r.results[0]["out_0"].reshape(shape)
```
